# Optimizing a Trainium2 kernel written in Bass

```python
import numpy as np
import jax
import jax.numpy as jnp

def _softmax(x, axis=-1):
    return jax.nn.softmax(x, axis=axis)

def _gelu(x):
    return jax.nn.gelu(x, approximate=True)

def _silu(x):
    return jax.nn.silu(x)

def _sigmoid(x):
    return jax.nn.sigmoid(x)

def _layernorm(x, axis=-1, eps=1e-05):
    m = jnp.mean(x, axis=axis, keepdims=True)
    v = jnp.var(x, axis=axis, keepdims=True)
    return (x - m) / jnp.sqrt(v + eps)

def _scatter_add(tgt, idx, src, axis=0):
    return tgt.at[idx].add(src)

def _segment_sum(src, seg, n):
    return jax.ops.segment_sum(src, seg, n)
kernel_name = 'mk_recurrent_d1_jaxref_r4_e95467'

def setup_inputs(seed: int=0):
    np.random.seed(seed)
    _w = jnp.asarray

    def _L0_attn_setup():
        import jax, jax.numpy as jnp
        import numpy as np
        NUM_HEADS = 16
        GROUP_SIZE = 4
        DIM = 256
        HEAD_DIM = DIM // NUM_HEADS
        NUM_GROUPS = max(1, NUM_HEADS // GROUP_SIZE)
        SCALE = HEAD_DIM ** (-0.5)
        key = jax.random.key(seed)
        k1, k2, k3, k4, k5 = jax.random.split(key, 5)
        B, T = (1, 1024)
        x = jax.random.normal(k1, (B, T, DIM), dtype=jnp.float32)
        Wq = jax.random.normal(k2, (DIM, NUM_HEADS * HEAD_DIM), dtype=jnp.float32) * DIM ** (-0.5)
        Wk = jax.random.normal(k3, (DIM, NUM_GROUPS * HEAD_DIM), dtype=jnp.float32) * DIM ** (-0.5)
        Wv = jax.random.normal(k4, (DIM, NUM_GROUPS * HEAD_DIM), dtype=jnp.float32) * DIM ** (-0.5)
        Wo = jax.random.normal(k5, (NUM_HEADS * HEAD_DIM, DIM), dtype=jnp.float32) * DIM ** (-0.5)
        return {'x': x, 'Wq': Wq, 'Wk': Wk, 'Wv': Wv, 'Wo': Wo}
    _L0_attn_in = _L0_attn_setup()

    def _L0_ffn_setup():
        import jax, jax.numpy as jnp
        import numpy as np
        DIM = 256
        HIDDEN = 768
        SCALE = 1.0 / 127.0

        def _dequant(w_int, dtype):
            return w_int.astype(dtype) * jnp.asarray(SCALE, dtype)
        key = jax.random.key(seed)
        k_x, k_g, k_u, k_d = jax.random.split(key, 4)
        x = jax.random.normal(k_x, (4, 512, DIM), dtype=jnp.float32)
        w_gate = jax.random.randint(k_g, (HIDDEN, DIM), -127, 128, dtype=jnp.int32)
        w_up = jax.random.randint(k_u, (HIDDEN, DIM), -127, 128, dtype=jnp.int32)
        w_down = jax.random.randint(k_d, (DIM, HIDDEN), -127, 128, dtype=jnp.int32)
        return {'x': x, 'w_gate': w_gate, 'w_up': w_up, 'w_down': w_down}
    _L0_ffn_in = _L0_ffn_setup()
    _d = {'L0_attn_x': _L0_attn_in['x'], 'L0_attn_Wq': _L0_attn_in['Wq'], 'L0_attn_Wk': _L0_attn_in['Wk'], 'L0_attn_Wv': _L0_attn_in['Wv'], 'L0_attn_Wo': _L0_attn_in['Wo'], 'L0_ffn_w_gate': _L0_ffn_in['w_gate'], 'L0_ffn_w_up': _L0_ffn_in['w_up'], 'L0_ffn_w_down': _L0_ffn_in['w_down']}
    _x0 = _d['L0_attn_x']
    _d['L0_attn_x'] = jax.random.normal(jax.random.fold_in(jax.random.key(seed), 1), (16, 1024, 256), dtype=_x0.dtype)
    del _x0
    return _d

def reference(L0_attn_x, L0_attn_Wq, L0_attn_Wk, L0_attn_Wv, L0_attn_Wo, L0_ffn_w_gate, L0_ffn_w_up, L0_ffn_w_down):

    def _L0_attn_ref(x, Wq, Wk, Wv, Wo):
        import jax, jax.numpy as jnp
        import numpy as np
        NUM_HEADS = 16
        GROUP_SIZE = 4
        DIM = 256
        HEAD_DIM = DIM // NUM_HEADS
        NUM_GROUPS = max(1, NUM_HEADS // GROUP_SIZE)
        SCALE = HEAD_DIM ** (-0.5)
        B, T, C = x.shape
        rep = NUM_HEADS // NUM_GROUPS
        q = (x @ Wq).reshape(B, T, NUM_HEADS, HEAD_DIM)
        k = (x @ Wk).reshape(B, T, NUM_GROUPS, HEAD_DIM)
        v = (x @ Wv).reshape(B, T, NUM_GROUPS, HEAD_DIM)
        k = jnp.repeat(k, rep, axis=2)
        v = jnp.repeat(v, rep, axis=2)
        scores = jnp.einsum('bqhd,bkhd->bhqk', q, k) * SCALE
        weights = jax.nn.softmax(scores, axis=-1)
        out = jnp.einsum('bhqk,bkhd->bqhd', weights, v)
        out = out.reshape(B, T, NUM_HEADS * HEAD_DIM)
        return out @ Wo

    def _L0_ffn_ref(x, w_gate, w_up, w_down):
        import jax, jax.numpy as jnp
        import numpy as np
        DIM = 256
        HIDDEN = 768
        SCALE = 1.0 / 127.0

        def _dequant(w_int, dtype):
            return w_int.astype(dtype) * jnp.asarray(SCALE, dtype)
        wg = _dequant(w_gate, x.dtype)
        wu = _dequant(w_up, x.dtype)
        wd = _dequant(w_down, x.dtype)
        gate = jnp.einsum('bsd,hd->bsh', x, wg)
        up = jnp.einsum('bsd,hd->bsh', x, wu)
        h = jax.nn.silu(gate) * up
        return jnp.einsum('bsh,dh->bsd', h, wd)
    x = L0_attn_x
    xn = _layernorm(x, axis=-1)
    s = _L0_attn_ref(xn, L0_attn_Wq, L0_attn_Wk, L0_attn_Wv, L0_attn_Wo)
    g = _silu(_L0_ffn_ref(xn, L0_ffn_w_gate, L0_ffn_w_up, L0_ffn_w_down))
    x = x + s * g
    return x

_drawn_inputs = setup_inputs


def setup_inputs(seed=0):
    import zlib

    import numpy as np

    out = dict(_drawn_inputs(seed))
    spreads = {}
    factors = {}
    for name, (base, spread) in spreads.items():
        noise = np.random.default_rng([zlib.crc32(name.encode()), seed]).standard_normal(out[name].shape)
        drawn = base * np.exp(spread * noise) if base else spread * noise
        out[name] = jnp.asarray(drawn.astype(out[name].dtype))
    for name, factor in factors.items():
        out[name] = (out[name] * factor).astype(out[name].dtype)
    return out
```

```python
from contextlib import ExitStack

import concourse.bass as bass
from concourse import mybir

ALU = mybir.AluOpType
ACT = mybir.ActivationFunctionType
AX = mybir.AxisListType
F32 = mybir.dt.float32
BF16 = mybir.dt.bfloat16
F16 = mybir.dt.float16
I32 = mybir.dt.int32

P = 128
BANK = 512
HEADS, GROUPS, HEAD_DIM = 16, 4, 16
PER_GROUP = HEADS // GROUPS
EPS = 1e-5
WEIGHT_SCALE = 1.0 / 127.0
SCORE_SCALE = HEAD_DIM ** -0.5

TERMS = [(0, 0), (0, 1), (0, 2), (1, 0), (1, 1), (2, 0)]
STACK = len(TERMS) * HEAD_DIM
ROWS = STACK + 3


def project(nc, psum, ident, x, w_q, w_k, w_v, w_gate_t, w_up_t, w_down_t, q_parts, k_parts, v_out, gate_out):
    tokens, dim = x.shape
    hidden = w_gate_t.shape[1]
    T = BANK // P
    CHUNKS = tokens // BANK
    KD = dim // P
    KH = hidden // P
    KV = GROUPS * HEAD_DIM
    PROJ = [(2, BANK), (3, BANK), (0, BANK // 2)]
    V_BANK = 1
    TURN = KH - 2
    EXACT = 128
    XN_SCALE = 2.0 ** 8
    H_SCALE = 2.0 ** -8
    assert (dim * EXACT) * WEIGHT_SCALE * (dim * EXACT) * H_SCALE < 65504
    assert dim ** 0.5 * XN_SCALE < 65504
    assert 2 * KV == P and KD == 2 and CHUNKS % 2 == 0 and CHUNKS >= 4 and T * KV <= BANK

    x_v = x.rearrange("(c t p) d -> c p t d", t=T, p=P)
    gate_v = gate_out.rearrange("(c t p) d -> c p t d", t=T, p=P)
    v_v = v_out.rearrange("(c t p) d -> c p t d", t=T, p=P)
    q_v = q_parts.rearrange("a (r p) (c n) -> c r p a n", p=P, n=BANK)
    k_v = k_parts.rearrange("a p (c s n) -> c s p a n", s=2, n=BANK // 2)

    with ExitStack() as ctx:
        def sb(name, shape, dt=F32):
            return ctx.enter_context(nc.sbuf_tensor(name, shape, dt))

        def sem(name):
            return ctx.enter_context(nc.semaphore(name))

        wq = sb("wq", [P, KD, dim])
        wk = sb("wk", [P, KD, KV])
        wv = sb("wv", [P, KD, KV])
        w_int = sb("w_int", [P, 3, KD * hidden], I32)
        w_full = sb("w_full", [P, 3, KD * hidden])
        w_half = sb("w_half", [P, 3, KD * hidden], F16)
        w_largest = sb("w_largest", [P, 1])
        w_largest_all = sb("w_largest_all", [1, 1])
        w_large = sb("w_large", [1, 1], I32)
        x_t = sb("x_t", [P, 2, T, dim])
        stats = sb("stats", [P, T, 6])
        moments = sb("moments", [P, T, 2])
        var_eps = sb("var_eps", [P, T])
        minus_half = sb("minus_half", [P, T])
        eps = sb("eps", [P, T])
        pause = sb("pause", [P, 1])
        rsqrt = sb("rsqrt", [P, T])
        rstd = sb("rstd", [P, T])
        xn_scale = sb("xn_scale", [P, T])
        xn = sb("xn", [P, T, dim])
        xn_t = sb("xn_t", [P, 2, KD, BANK])
        xn_high = sb("xn_high", [P, 2, KD, BANK], F16)
        xn_low = sb("xn_low", [P, 2, KD, BANK], F16)
        parts = sb("parts", [P, 3, 3, BANK], BF16)
        rest = sb("rest", [P, 3, BANK])
        v_t = sb("v_t", [P, T, KV])
        silu_gate = sb("silu_gate", [P, 2, BANK])
        h_t = sb("h_t", [P, KH, BANK])
        h_high = sb("h_high", [P, KH, BANK], F16)
        h_low = sb("h_low", [P, KH, BANK], F16)
        gate_t = sb("gate_t", [P, T, dim])

        def views(w):
            return (w[:, 0].rearrange("p (k n) -> p k n", k=KD), w[:, 1].rearrange("p (k n) -> p k n", k=KD),
                    w[:, 2].rearrange("p (k n) -> p k n", k=KH))

        proj_weights_in = sem("proj_weights_in")
        proj_weights_scaled = sem("proj_weights_scaled")
        ffn_weights_in = sem("ffn_weights_in")
        weights_ready = sem("weights_ready")
        largest_done = sem("largest_done")
        largest_turned = sem("largest_turned")
        large_known = sem("large_known")
        consts_ready = sem("consts_ready")
        x_in = [sem("x_in_even"), sem("x_in_odd")]
        stats_chain = sem("stats_chain")
        stats_done = sem("stats_done")
        var_done = sem("var_done")
        rsqrt_done = sem("rsqrt_done")
        rstd_done = sem("rstd_done")
        xn_done = sem("xn_done")
        turned = sem("turned")
        xn_t_done = sem("xn_t_done")
        xn_low_done = sem("xn_low_done")
        proj_done = sem("proj_done")
        high_done = sem("high_done")
        rest_done = sem("rest_done")
        mid_done = sem("mid_done")
        low_done = sem("low_done")
        v_done = sem("v_done")
        gate_up_done = sem("gate_up_done")
        silu_done = sem("silu_done")
        h_done = sem("h_done")
        h_high_done = sem("h_high_done")
        h_low_done = sem("h_low_done")
        down_done = sem("down_done")
        gate_done = sem("gate_done")
        qk_stored = sem("qk_stored")
        v_stored = sem("v_stored")
        gate_stored = sem("gate_stored")
        QK_STORES = 4 * 16

        turned0, xn_t0, v0, gate0, gate_up0, h0, h_low0, rest0, low0, down0 = 1, 1, 1, 4, 2 * KH, 2, 1, 1, 3, 1
        stored0 = 16

        block = ctx.enter_context(nc.Block())

        def pairs(engine, pair):
            with engine.Fori(0, CHUNKS // 2 - 1) as i:
                pair(i, False)
            pair(CHUNKS // 2 - 1, True)

        @block.sync
        def _(sp):
            sp.sem_inc(qk_stored, stored0)
            sp.sem_inc(v_stored, stored0)
            sp.sem_inc(gate_stored, stored0)

            def store_projections(n):
                for r in range(3):
                    sp.wait_ge(low_done, 3 * n + r + 1 + low0)
                    if r < 2:
                        sp.dma_start(q_v[n, r], parts[:, r]).then_inc(qk_stored, 16)
                    else:
                        for s in range(2):
                            sp.dma_start(k_v[n, s], parts[s * KV:(s + 1) * KV, r, :, 0:BANK // 2]).then_inc(qk_stored, 16)
                sp.wait_ge(v_done, n + 1 + v0)
                sp.dma_start(v_v[n], v_t[:]).then_inc(v_stored, 16)

            def pair(i, last):
                for sub in range(2):
                    c = 2 * i + sub
                    if not last:
                        sp.wait_ge(xn_done, c + 1)
                        sp.dma_start(x_t[:, sub], x_v[c + 2]).then_inc(x_in[sub], 16)
                    if not (last and sub == 1):
                        store_projections(c + 1)
                    sp.wait_ge(gate_done, 2 * c + 2 + gate0)
                    sp.dma_start(gate_v[c], gate_t[:]).then_inc(gate_stored, 16)

            sp.dma_start(x_t[:, 0], x_v[0]).then_inc(x_in[0], 16)
            sp.dma_start(wq[:], w_q.rearrange("(k p) n -> p k n", p=P)).then_inc(proj_weights_in, 16)
            sp.dma_start(wk[:], w_k.rearrange("(k p) n -> p k n", p=P)).then_inc(proj_weights_in, 16)
            sp.dma_start(wv[:], w_v.rearrange("(k p) n -> p k n", p=P)).then_inc(proj_weights_in, 16)
            for dst, w in zip(views(w_int), (w_gate_t, w_up_t, w_down_t)):
                sp.dma_start(dst, w.rearrange("(k p) n -> p k n", p=P)).then_inc(ffn_weights_in, 16)
            sp.dma_start(x_t[:, 1], x_v[1]).then_inc(x_in[1], 16)
            store_projections(0)
            pairs(sp, pair)
            sp.wait_ge(qk_stored, QK_STORES * CHUNKS + stored0)
            sp.wait_ge(v_stored, 16 * CHUNKS + stored0)
            sp.wait_ge(gate_stored, 16 * CHUNKS + stored0)

        @block.vector
        def _(dve):
            dve.sem_inc(h_done, h0)
            dve.sem_inc(rest_done, rest0)
            nc.vector.memset(minus_half[:], -0.5).then_inc(consts_ready, 1)
            nc.vector.memset(eps[:], EPS).then_inc(consts_ready, 1)
            nc.vector.memset(xn_scale[:], XN_SCALE).then_inc(consts_ready, 1)

            def normalise(n, lap, sub):
                dve.wait_ge(x_in[sub], 16 * lap + 16)
                for t in range(T):
                    ins = nc.vector.bn_stats(stats[:, t], x_t[:, sub, t])
                ins.then_inc(stats_chain, 1)
                dve.wait_ge(stats_chain, n + 1)
                nc.vector.memset(pause[:], 0.0)
                for t in range(T):
                    ins = nc.vector.bn_aggr(moments[:, t], stats[:, t])
                ins.then_inc(stats_done, 1)
                dve.wait_ge(rstd_done, n + 1)
                dve.wait_ge(turned, 2 * n + turned0)
                for t in range(T):
                    ins = nc.vector.tensor_scalar(xn[:, t], x_t[:, sub, t], moments[:, t, 0:1], rstd[:, t:t + 1],
                                                  ALU.subtract, ALU.mult)
                ins.then_inc(xn_done, 1)

            def split_projections(n):
                for r, (bank, w) in enumerate(PROJ):
                    dve.wait_ge(high_done, 3 * n + r + 1)
                    dve.wait_ge(low_done, 3 * (n - 1) + r + 1 + low0)
                    nc.vector.tensor_tensor(rest[:, r, 0:w], psum[:, bank, 0:w], parts[:, r, 0, 0:w],
                                            ALU.subtract).then_inc(rest_done, 1)
                    dve.wait_ge(rest_done, 3 * n + r + 1 + rest0)
                    nc.vector.tensor_copy(parts[:, r, 1, 0:w], rest[:, r, 0:w]).then_inc(mid_done, 1)

            def hidden_values(c, m):
                dve.wait_ge(silu_done, KH * c + m + 1)
                if m == 0:
                    dve.wait_ge(h_low_done, KH * c + h_low0)
                    dve.wait_ge(down_done, 2 * c + down0)
                nc.vector.scalar_tensor_tensor(h_t[:, m], psum[:, 5 + 2 * (m % 2)], H_SCALE / XN_SCALE, silu_gate[:, m % 2],
                                               ALU.mult, ALU.mult).then_inc(h_done, 1)
                dve.wait_ge(h_done, KH * c + m + 1 + h0)
                nc.vector.tensor_copy(h_high[:, m], h_t[:, m]).then_inc(h_high_done, 1)

            def pair(i, last):
                for sub in range(2):
                    c, ahead = 2 * i + sub, not (last and sub == 1)
                    if ahead:
                        normalise(c + 1, i + sub, 1 - sub)
                    for m in range(KH):
                        hidden_values(c, m)
                    if ahead:
                        split_projections(c + 1)

            normalise(0, 0, 0)
            dve.wait_ge(proj_weights_in, 3 * 16)
            for w in (wq, wk, wv):
                nc.vector.tensor_scalar(w[:], w[:], 1.0 / XN_SCALE, None, ALU.mult).then_inc(proj_weights_scaled, 1)
            dve.wait_ge(ffn_weights_in, 3 * 16)
            nc.vector.tensor_reduce(w_largest[:], w_int[:].rearrange("p w n -> p (w n)"), AX.X, ALU.max,
                                    apply_absolute_value=True).then_inc(largest_done, 1)
            nc.vector.tensor_copy(w_full[:], w_int[:]).then_inc(weights_ready, 1)
            dve.wait_ge(weights_ready, 1)
            nc.vector.tensor_copy(w_half[:], w_full[:]).then_inc(weights_ready, 1)
            split_projections(0)
            dve.wait_ge(largest_turned, 1)
            nc.vector.tensor_reduce(w_largest_all[:], psum[0:1, 7, 0:P], AX.X, ALU.max).then_inc(largest_done, 1)
            dve.wait_ge(largest_done, 2)
            nc.vector.tensor_scalar(w_large[:], w_largest_all[:], float(EXACT), None,
                                    ALU.is_gt).then_inc(large_known, 1)
            pairs(dve, pair)

        @block.gpsimd
        def _(pool):
            pool.sem_inc(low_done, low0)
            pool.sem_inc(h_low_done, h_low0)

            def rstd_of(n):
                pool.wait_ge(stats_done, n + 1)
                nc.gpsimd.tensor_tensor(var_eps[:], moments[:, :, 1], eps[:], ALU.add).then_inc(var_done, 1)
                pool.wait_ge(var_done, n + 1)
                nc.gpsimd.tensor_tensor(rsqrt[:], var_eps[:], minus_half[:], ALU.pow).then_inc(rsqrt_done, 1)
                pool.wait_ge(rsqrt_done, n + 1)
                nc.gpsimd.tensor_tensor(rstd[:], rsqrt[:], xn_scale[:], ALU.mult).then_inc(rstd_done, 1)

            def low_of_xn(n, sub):
                for k in range(KD):
                    pool.wait_ge(xn_t_done, 2 * KD * n + KD + k + 1 + xn_t0)
                    nc.gpsimd.tensor_tensor(xn_low[:, sub, k], xn_t[:, sub, k], xn_high[:, sub, k],
                                            ALU.subtract).then_inc(xn_low_done, 1)

            def low_of_projections(n):
                for r, (_, w) in enumerate(PROJ):
                    pool.wait_ge(mid_done, 3 * n + r + 1)
                    nc.gpsimd.tensor_tensor(parts[:, r, 2, 0:w], rest[:, r, 0:w], parts[:, r, 1, 0:w],
                                            ALU.subtract).then_inc(low_done, 1)

            def low_of_hidden(c, m):
                pool.wait_ge(h_high_done, KH * c + m + 1)
                nc.gpsimd.tensor_tensor(h_low[:, m], h_t[:, m], h_high[:, m], ALU.subtract).then_inc(h_low_done, 1)

            def pair(i, last):
                for sub in range(2):
                    c, ahead = 2 * i + sub, not (last and sub == 1)
                    if ahead:
                        rstd_of(c + 1)
                    for m in range(KH - 1):
                        low_of_hidden(c, m)
                    if ahead:
                        low_of_xn(c + 1, 1 - sub)
                    low_of_hidden(c, KH - 1)
                    if ahead:
                        low_of_projections(c + 1)

            pool.wait_ge(consts_ready, 3)
            rstd_of(0)
            low_of_xn(0, 0)
            low_of_projections(0)
            pairs(pool, pair)

        @block.tensor
        def _(pe):
            pe.sem_inc(turned, turned0)
            pe.sem_inc(gate_up_done, gate_up0)
            pe.sem_inc(down_done, down0)

            def turn_xn(n):
                pe.wait_ge(xn_done, n + 1)
                pe.wait_ge(rest_done, 3 * n + rest0)
                pe.wait_ge(v_done, n + v0)
                for k in range(KD):
                    for t in range(T):
                        ins = pe.transpose(psum[:, k, t * P:(t + 1) * P], xn[:, t, k * P:(k + 1) * P], ident[:])
                    ins.then_inc(turned, 1)

            def project_chunk(n, sub):
                pe.wait_ge(xn_t_done, 2 * KD * n + KD + xn_t0)
                for r in range(2):
                    bank = PROJ[r][0]
                    pe.wait_ge(gate_done, 2 * (n - 2) + r + 1 + gate0)
                    for k in range(KD):
                        ins = pe.matmul(psum[:, bank], wq[:, k, r * P:(r + 1) * P], xn_t[:, sub, k],
                                        start=(k == 0), stop=(k == KD - 1))
                    ins.then_inc(proj_done, 1)
                pe.wait_ge(xn_t_done, 2 * KD * (n + 1) + xn_t0)
                bank, w = PROJ[2]
                for k in range(KD):
                    for s in range(2):
                        ins = pe.matmul(psum[s * KV:(s + 1) * KV, bank, 0:w], wk[:, k],
                                        xn_t[:, sub, k, s * w:(s + 1) * w], start=(k == 0), stop=(k == KD - 1))
                ins.then_inc(proj_done, 1)
                for t in range(T):
                    for k in range(KD):
                        ins = pe.matmul(psum[:, V_BANK, t * KV:(t + 1) * KV], xn_t[:, sub, k, t * P:(t + 1) * P],
                                        wv[:, k], start=(k == 0), stop=(k == KD - 1))
                ins.then_inc(proj_done, 1)

            def accumulate(out, products):
                for n, (lhs, rhs) in enumerate(products):
                    ins = pe.matmul(out, lhs, rhs, start=(n == 0), stop=(n == len(products) - 1))
                return ins

            def gate_up(c, m, sub, large):
                pe.wait_ge(h_done, KH * c + m - 1 + h0)
                hid = slice(m * P, (m + 1) * P)
                for w in range(2):
                    if large:
                        products = [(views(w_full)[w][:, k, hid], xn_t[:, sub, k]) for k in range(KD)]
                    else:
                        products = [(views(w_half)[w][:, k, hid], part[:, sub, k])
                                    for k in range(KD) for part in (xn_high, xn_low)]
                    ins = accumulate(psum[:, 4 + 2 * (m % 2) + w], products)
                ins.then_inc(gate_up_done, 1)

            def down(c, projected, large):
                pe.wait_ge(h_low_done, KH * (c + 1) + h_low0)
                for t in range(T):
                    if t % 2 == 0:
                        pe.wait_ge(rest_done, 3 * (projected - 1) + t // 2 + 1 + rest0)
                    tok = slice(t * P, (t + 1) * P)
                    if large:
                        products = [(h_t[:, m, tok], views(w_full)[2][:, m]) for m in range(KH)]
                    else:
                        products = [(part[:, m, tok], views(w_half)[2][:, m])
                                    for m in range(KH) for part in (h_high, h_low)]
                    ins = accumulate(psum[:, 2 + t // 2, (t % 2) * dim:(t % 2 + 1) * dim], products)
                    if t % 2 == 1:
                        ins.then_inc(down_done, 1)

            def chunks(large):
                def pair(i, last):
                    for sub in range(2):
                        c, ahead = 2 * i + sub, not (last and sub == 1)
                        pe.wait_ge(xn_low_done, KD * (c + 1))
                        for m in range(KH):
                            if m == TURN and ahead:
                                turn_xn(c + 1)
                            gate_up(c, m, sub, large)
                        if ahead:
                            project_chunk(c + 1, 1 - sub)
                        down(c, c + 1 + ahead, large)
                pairs(pe, pair)

            turn_xn(0)
            pe.wait_ge(proj_weights_scaled, 3)
            project_chunk(0, 0)
            pe.wait_ge(largest_done, 1)
            pe.transpose(psum[0:1, 7, 0:P], w_largest[:], ident[:]).then_inc(largest_turned, 1)
            pe.wait_ge(weights_ready, 2)
            pe.wait_ge(large_known, 1)
            large = pe.value_load(w_large[0:1, 0:1])
            with pe.If(large > 0):
                chunks(True)
            with pe.Else():
                chunks(False)

        @block.scalar
        def _(act):
            act.sem_inc(xn_t_done, xn_t0)
            act.sem_inc(v_done, v0)
            act.sem_inc(gate_done, gate0)
            act.preload_act_table(ACT.Silu)

            def copy_xn(n, sub):
                act.wait_ge(gate_up_done, KH * (n - 1) + gate_up0)
                for k in range(KD):
                    act.wait_ge(turned, 2 * n + k + 1 + turned0)
                    nc.scalar.copy(xn_t[:, sub, k], psum[:, k]).then_inc(xn_t_done, 1)
                for k in range(KD):
                    nc.scalar.copy(xn_high[:, sub, k], psum[:, k]).then_inc(xn_t_done, 1)

            def copy_projections(n):
                act.wait_ge(qk_stored, QK_STORES * n + stored0)
                for r, (bank, w) in enumerate(PROJ):
                    act.wait_ge(proj_done, 4 * n + r + 1)
                    nc.scalar.copy(parts[:, r, 0, 0:w], psum[:, bank, 0:w]).then_inc(high_done, 1)
                act.wait_ge(proj_done, 4 * n + 4)
                act.wait_ge(v_stored, 16 * n + stored0)
                nc.scalar.copy(v_t[:].rearrange("p t n -> p (t n)"), psum[:, V_BANK, 0:T * KV]).then_inc(v_done, 1)

            def silu_of_gate(c, m):
                act.wait_ge(gate_up_done, KH * c + m + 1 + gate_up0)
                act.wait_ge(h_done, KH * c + m - 1 + h0)
                nc.scalar.activation(silu_gate[:, m % 2], psum[:, 4 + 2 * (m % 2)], ACT.Silu,
                                     scale=WEIGHT_SCALE / XN_SCALE).then_inc(silu_done, 1)

            def pair(i, last):
                for sub in range(2):
                    c, ahead = 2 * i + sub, not (last and sub == 1)
                    for m in range(KH):
                        if m == TURN and ahead:
                            copy_xn(c + 1, 1 - sub)
                        silu_of_gate(c, m)
                    if ahead:
                        copy_projections(c + 1)
                    act.wait_ge(gate_stored, 16 * c + stored0)
                    for n in range(2):
                        act.wait_ge(down_done, 2 * c + n + 1 + down0)
                        nc.scalar.activation(gate_t[:, 2 * n:2 * n + 2].rearrange("p t d -> p (t d)"),
                                             psum[:, 2 + n], ACT.Silu,
                                             scale=WEIGHT_SCALE * WEIGHT_SCALE / H_SCALE).then_inc(gate_done, 1)

            copy_xn(0, 0)
            copy_projections(0)
            pairs(act, pair)


def attend(nc, psum, ident, x, w_o, q_parts, k_parts, v_in, gate_in, out, batches):
    tokens, dim = x.shape
    seq = tokens // batches
    KT = seq // P
    HALVES = seq // BANK
    QT = BANK // P
    HALF_STEPS = GROUPS * HALVES
    SLOTS = HALF_STEPS * KT
    UNITS = PER_GROUP * QT
    S_BANKS, O_BANK, RING_BANK = 3, 3, 4
    LAG = 2
    NR = 4
    assert HALVES == 2 and PER_GROUP == 4 and KT == 2 * QT and dim == 2 * P and batches >= 3

    x_v = x.rearrange("(b t p) d -> b p t d", t=KT, p=P)
    gate_v = gate_in.rearrange("(b t p) d -> b p t d", t=KT, p=P)
    out_v = out.rearrange("(b t p) d -> b p t d", t=KT, p=P)
    q_v = q_parts.rearrange("a (g j d) (b n) -> a b g d j n", g=GROUPS, d=HEAD_DIM, n=seq)
    k_v = k_parts.rearrange("a (g d) (b n) -> a b g d n", g=GROUPS, n=seq)
    v_v = v_in.rearrange("(b t p) (g d) -> b g p t d", t=KT, p=P, g=GROUPS)

    END = ("outputs", "norm1", "project1")

    def turns(hs, kt, first, last):
        found = []
        if kt == 2 and not (last and hs == HALF_STEPS - 1):
            found.append("max")
        if kt == 5 and not (first and hs == 0):
            found.append("outputs")
        if hs == 1 and not first:
            found += {1: ["norm0"], 3: ["norm1"], 4: ["project0"], 6: ["project1"]}.get(kt, [])
        if last and hs == HALF_STEPS - 1:
            found += {6: ["norm0"], 7: ["project0"]}.get(kt, [])
        return found

    def has_maxima(hs, last):
        return not (last and hs // HALVES == GROUPS - 1)

    def ring_use(first, last, name=None, since=0):
        n = 0
        for hs in range(HALF_STEPS):
            for kt in range(KT):
                n += has_maxima(hs, last)
                for turn in turns(hs, kt, first, last):
                    if turn == name and hs >= since:
                        return n
                    n += 1
                n += has_maxima(hs, last)
        return n

    RING_PROLOGUE = HALVES * UNITS + 1
    RING_FIRST = ring_use(True, False)
    RING_BATCH = ring_use(False, False)
    assert RING_BATCH % 2 == 0

    def ring_start(b, first):
        return (0, RING_PROLOGUE) if first else (RING_BATCH * (b - 1), RING_PROLOGUE + RING_FIRST)

    def ring_bank(at):
        return RING_BANK + 2 * (at % 2)

    with ExitStack() as ctx:
        def sb(name, shape, dt=F32):
            return ctx.enter_context(nc.sbuf_tensor(name, shape, dt))

        def sem(name):
            return ctx.enter_context(nc.semaphore(name))

        q_stack = sb("q_stack", [P, GROUPS, HALVES, PER_GROUP * BANK], BF16)
        k_stack = sb("k_stack", [P, GROUPS, seq], BF16)
        v_ones = sb("v_ones", [P, GROUPS, KT, 2 * HEAD_DIM])
        wo = sb("wo", [P, 2, dim])
        probs = sb("probs", [P, NR, PER_GROUP, BANK])
        minus_max = sb("minus_max", [P, HALVES, UNITS])
        max_rest = sb("max_rest", [UNITS, HALVES, P])
        max_parts = sb("max_parts", [UNITS, HALVES, 3, P], BF16)
        o_sum = sb("o_sum", [P, BANK])
        inv_sum = sb("inv_sum", [P, QT, PER_GROUP])
        o_norm = sb("o_norm", [P, KT, dim])
        o_norm_t = sb("o_norm_t", [P, 2, seq])
        x_b = sb("x_b", [P, KT, dim])
        gate_b = sb("gate_b", [P, KT, dim])
        y_b = sb("y_b", [P, KT, dim])

        ready = sem("ready")
        wo_in = sem("wo_in")
        loaded = [sem(f"loaded{g}") for g in range(GROUPS)]
        residual_in = sem("residual_in")
        max_in = [sem("max_in0"), sem("max_in1")]
        scores_done = sem("scores_done")
        exp_done = sem("exp_done")
        max_scores_done = sem("max_scores_done")
        max_turned = sem("max_turned")
        split_chain = sem("split_chain")
        max_split = sem("max_split")
        av_done = sem("av_done")
        o_copied = sem("o_copied")
        o_turned = sem("o_turned")
        inv_done = sem("inv_done")
        norm_turned = sem("norm_turned")
        y_done = sem("y_done")
        ring_free = sem("ring_free")
        summed = sem("summed")
        stored = sem("stored")

        LOADS = (HALVES + 1) * len(TERMS) + 1
        exp0, ring0, av0, copied0, turned0, summed0, stored0, max_in0 = S_BANKS, 2, NR, 1, 1, 1, 16, 16

        block = ctx.enter_context(nc.Block())

        @block.sync
        def _(sp):
            sp.sem_inc(stored, stored0)
            for half in range(HALVES):
                sp.sem_inc(max_in[half], max_in0)

            def load_step(b, g):
                for t, (a, c) in enumerate(TERMS):
                    rows = slice(t * HEAD_DIM, (t + 1) * HEAD_DIM)
                    for half in range(HALVES):
                        sp.dma_start(q_stack[rows, g, half].rearrange("d (j n) -> d j n", n=BANK),
                                     q_v[a, b, g, :, :, half * BANK:(half + 1) * BANK]).then_inc(loaded[g], 16)
                    sp.dma_start(k_stack[rows, g], k_v[c, b, g]).then_inc(loaded[g], 16)
                sp.dma_start(v_ones[:, g, :, 0:HEAD_DIM], v_v[b, g]).then_inc(loaded[g], 16)

            def send_max(half, g, n):
                sp.wait_ge(max_split, n + 1)
                for a in range(3):
                    sp.dma_start(q_stack[STACK + a:STACK + a + 1, g, half],
                                 max_parts[:, half, a]).then_inc(max_in[half], 16)

            def batch(b, first, last):
                for g in range(GROUPS):
                    if not (last and g > 0):
                        sp.wait_ge(av_done, SLOTS * b + HALVES * KT * g + av0)
                        load_step(b + (g > 0), (g + GROUPS - 1) % GROUPS)
                    for half in range(HALVES):
                        hs = HALVES * g + half
                        if "max" in turns(hs, 2, first, last):
                            send_max(1 - half, (g + half) % GROUPS, HALF_STEPS * b + hs + 1)
                        if hs == HALVES:
                            sp.wait_ge(summed, 2 * b + summed0)
                            if not first:
                                sp.dma_start(out_v[b - 1], y_b[:]).then_inc(stored, 16)
                            sp.dma_start(x_b[:], x_v[b]).then_inc(residual_in, 16)
                            sp.dma_start(gate_b[:], gate_v[b]).then_inc(residual_in, 16)

            load_step(0, 0)
            sp.dma_start(wo[:], w_o.rearrange("(k p) n -> p k n", p=P)).then_inc(wo_in, 16)
            for g in range(1, GROUPS - 1):
                load_step(0, g)
            send_max(0, 0, 0)
            batch(0, True, False)
            with sp.Fori(1, batches - 1) as b:
                batch(b, False, False)
            batch(batches - 1, False, True)
            for hq in range(2):
                sp.wait_ge(summed, 2 * batches - 1 + hq + summed0)
                tiles = slice(hq * QT, (hq + 1) * QT)
                sp.dma_start(out_v[batches - 1][:, tiles], y_b[:, tiles]).then_inc(stored, 16)
            sp.wait_ge(stored, 16 * (batches + 1) + stored0)

        @block.tensor
        def _(pe):
            pe.sem_inc(av_done, av0)

            def max_scores(g, half, unit, use, at):
                j, qt = unit // QT, unit % QT
                q0 = j * BANK + qt * P
                pe.wait_ge(ring_free, use - 1 + ring0)
                for kh in range(HALVES):
                    ins = pe.matmul(psum[:, ring_bank(at) + kh], q_stack[0:STACK, g, half, q0:q0 + P],
                                    k_stack[0:STACK, g, kh * BANK:(kh + 1) * BANK], start=True, stop=True)
                ins.then_inc(max_scores_done, 1)

            def scores(slot, g, half, kt, j, at):
                n = PER_GROUP * at + j
                pe.wait_ge(exp_done, PER_GROUP * slot + (0 if n == 0 else j - S_BANKS + 1) + exp0)
                pe.matmul(psum[:, n % S_BANKS], k_stack[0:ROWS, g, kt * P:(kt + 1) * P],
                          q_stack[0:ROWS, g, half, j * BANK:(j + 1) * BANK],
                          start=True, stop=True).then_inc(scores_done, 1)

            def weighted_values(b, at):
                slot, kt, g = SLOTS * b + at, at % KT, at % SLOTS // KT // HALVES
                pe.wait_ge(exp_done, PER_GROUP * (slot + 1) + exp0)
                if kt == 0:
                    pe.wait_ge(o_copied, HALF_STEPS * b + at // KT + copied0)
                for j in range(PER_GROUP):
                    ins = pe.matmul(psum[32 * j:32 * j + 32, O_BANK], v_ones[:, g, kt], probs[:, kt % NR, j],
                                    start=(kt == 0), stop=(kt == KT - 1))
                ins.then_inc(av_done, 1)

            def turn(name, n_half, use, at, settled):
                bank = ring_bank(at)
                pe.wait_ge(ring_free, use - (0 if settled else 1) + ring0)
                if name == "outputs":
                    pe.wait_ge(o_copied, n_half + copied0)
                    for qt in range(QT):
                        ins = pe.transpose(psum[:, bank, qt * P:(qt + 1) * P], o_sum[:, qt * P:(qt + 1) * P], ident[:])
                    ins.then_inc(o_turned, 1)
                elif name.startswith("norm"):
                    hq = int(name[-1])
                    for k in range(2):
                        for qt in range(QT):
                            ins = pe.transpose(psum[:, bank + k, qt * P:(qt + 1) * P],
                                               o_norm[:, hq * QT + qt, k * P:(k + 1) * P], ident[:])
                    ins.then_inc(norm_turned, 1)
                else:
                    hq = int(name[-1])
                    for t in range(QT):
                        tile = hq * QT + t
                        for k in range(2):
                            ins = pe.matmul(psum[:, bank + t // 2, (t % 2) * dim:(t % 2 + 1) * dim],
                                            o_norm_t[:, k, tile * P:(tile + 1) * P], wo[:, k],
                                            start=(k == 0), stop=(k == 1))
                    ins.then_inc(y_done, 1)

            def batch(b, first, last):
                base, at = ring_start(b, first)
                for s in range(SLOTS):
                    hs, kt = s // KT, s % KT
                    g, half = hs // HALVES, hs % HALVES
                    n_half = HALF_STEPS * b + hs
                    if kt == 0:
                        pe.wait_ge(max_in[half], 3 * 16 * (GROUPS * b + g + 1) + max_in0)
                        if half == 0 and has_maxima(hs, last):
                            pe.wait_ge(loaded[(g + 1) % GROUPS], 16 * LOADS * (b + 1 + (g + 1) // GROUPS))
                    second = 3 if turns(hs, kt, first, last) else 2
                    for j in range(PER_GROUP):
                        scores(SLOTS * b + s, g, half, kt, j, s)
                        if j in (0, second) and has_maxima(hs, last):
                            max_scores((g + 1) % GROUPS, half, 2 * kt + (j > 0), base + at, at)
                            at += 1
                        if j == 1:
                            if s >= LAG or not first:
                                weighted_values(b, s - LAG)
                            for name in turns(hs, kt, first, last):
                                if name == "max":
                                    turn_max(half, base + at, at, not has_maxima(hs, last))
                                else:
                                    turn(name, n_half, base + at, at, not has_maxima(hs, last))
                                at += 1
                return base, at

            def turn_max(half, use, at, settled):
                pe.wait_ge(ring_free, use - (0 if settled else 1) + ring0)
                pe.transpose(psum[0:UNITS, ring_bank(at), 0:P], minus_max[:, 1 - half], ident[:]).then_inc(max_turned, 1)

            pe.wait_ge(ready, 2)
            pe.wait_ge(loaded[0], 16 * LOADS)
            for half in range(HALVES):
                for unit in range(UNITS):
                    max_scores(0, half, unit, half * UNITS + unit, half * UNITS + unit)
            turn_max(1, HALVES * UNITS, HALVES * UNITS, False)
            pe.wait_ge(wo_in, 16)
            batch(0, True, False)
            with pe.Fori(1, batches - 1) as b:
                batch(b, False, False)
            base, at = batch(batches - 1, False, True)
            for s in range(SLOTS, SLOTS + LAG):
                weighted_values(batches - 1, s - LAG)
            for name in END:
                turn(name, HALF_STEPS * batches, base + at, at, True)
                at += 1

        @block.scalar
        def _(act):
            act.sem_inc(exp_done, exp0)
            act.sem_inc(o_copied, copied0)
            act.sem_inc(o_turned, turned0)

            def copy_outputs(n_half):
                act.wait_ge(av_done, KT * (n_half + 1) + av0)
                act.wait_ge(o_turned, n_half + turned0)
                nc.scalar.copy(o_sum[:], psum[:, O_BANK]).then_inc(o_copied, 1)

            def batch(b, first):
                for s in range(SLOTS):
                    hs, kt = s // KT, s % KT
                    slot = SLOTS * b + s
                    act.wait_ge(av_done, slot - NR + 1 + av0)
                    for j in range(PER_GROUP):
                        act.wait_ge(scores_done, PER_GROUP * slot + j + 1)
                        nc.scalar.activation(probs[:, kt % NR, j], psum[:, (PER_GROUP * s + j) % S_BANKS],
                                             ACT.Exp, scale=SCORE_SCALE).then_inc(exp_done, 1)
                        if kt == LAG - 1 and j == 2 and not (first and hs == 0):
                            copy_outputs(HALF_STEPS * b + hs - 1)

            batch(0, True)
            with act.Fori(1, batches) as b:
                batch(b, False)
            copy_outputs(HALF_STEPS * batches - 1)

        @block.vector
        def _(dve):
            dve.sem_inc(ring_free, ring0)
            nc.vector.memset(k_stack[STACK:ROWS], 1.0).then_inc(ready, 1)
            nc.vector.memset(v_ones[:, :, :, HEAD_DIM:], 1.0).then_inc(ready, 1)

            def reduce_max(half, unit, n, at):
                dve.wait_ge(max_scores_done, n + 1)
                bank = ring_bank(at)
                nc.vector.tensor_reduce(minus_max[:, half, unit:unit + 1],
                                        psum[:, bank:bank + 2].rearrange("p a n -> p (a n)"), AX.X, ALU.max,
                                        negate=True).then_inc(ring_free, 1)

            def split_max(half, n, sent, use, at):
                dve.wait_ge(max_turned, n + 1)
                dve.wait_ge(max_in[half], 3 * 16 * sent + max_in0)
                turned = psum[0:UNITS, ring_bank(at), 0:P]
                nc.vector.tensor_copy(max_parts[:, half, 0], turned).then_inc(split_chain, 1)
                dve.wait_ge(split_chain, 2 * n + 1)
                nc.vector.tensor_tensor(max_rest[:, half], turned, max_parts[:, half, 0],
                                        ALU.subtract).then_inc(ring_free, 1)

            def mid_of_max(half, use):
                dve.wait_ge(ring_free, use + 1 + ring0)
                nc.vector.tensor_copy(max_parts[:, half, 1], max_rest[:, half]).then_inc(split_chain, 1)

            def low_of_max(half, n):
                dve.wait_ge(split_chain, 2 * n + 2)
                nc.vector.tensor_tensor(max_parts[:, half, 2], max_rest[:, half], max_parts[:, half, 1],
                                        ALU.subtract).then_inc(max_split, 1)

            def normalise(hs, n_half, use, at):
                g, half = hs // HALVES, hs % HALVES
                dve.wait_ge(ring_free, use + ring0)
                dve.wait_ge(o_turned, n_half + 1 + turned0)
                turned = psum[:, ring_bank(at)].rearrange("p (t j d) -> p t j d", j=PER_GROUP, d=2 * HEAD_DIM)
                nc.vector.reciprocal(inv_sum[:], turned[:, :, :, HEAD_DIM]).then_inc(inv_done, 1)
                dve.wait_ge(inv_done, n_half + 1)
                width = PER_GROUP * HEAD_DIM
                nc.vector.tensor_tensor(
                    o_norm[:, half * QT:(half + 1) * QT, g * width:(g + 1) * width]
                    .rearrange("p t (j d) -> p t j d", j=PER_GROUP),
                    turned[:, :, :, 0:HEAD_DIM],
                    inv_sum[:].unsqueeze(3).to_broadcast([P, QT, PER_GROUP, HEAD_DIM]),
                    ALU.mult).then_inc(ring_free, 1)

            def copy_norm(b, hq, at):
                dve.wait_ge(norm_turned, 2 * b + hq + 1)
                bank = ring_bank(at)
                nc.vector.tensor_copy(o_norm_t[:, :, hq * BANK:(hq + 1) * BANK],
                                      psum[:, bank:bank + 2]).then_inc(ring_free, 1)

            def gate(b, hq, at):
                if hq == 0:
                    dve.wait_ge(residual_in, 32 * (b + 1))
                    dve.wait_ge(stored, 16 * b + stored0)
                dve.wait_ge(y_done, 2 * b + hq + 1)
                bank, tiles = ring_bank(at), slice(hq * QT, (hq + 1) * QT)
                nc.vector.tensor_tensor(y_b[:, tiles].rearrange("p t d -> p (t d)"),
                                        psum[:, bank:bank + 2].rearrange("p a n -> p (a n)"),
                                        gate_b[:, tiles].rearrange("p t d -> p (t d)"),
                                        ALU.mult).then_inc(ring_free, 1)

            def end_of_batch(name, b, use, at):
                if name == "outputs":
                    normalise(HALF_STEPS - 1, HALF_STEPS * (b + 1) - 1, use, at)
                elif name.startswith("norm"):
                    copy_norm(b, int(name[-1]), at)
                else:
                    gate(b, int(name[-1]), at)

            def batch(b, first, last):
                base, at = ring_start(b, first)
                for s in range(SLOTS):
                    hs, kt = s // KT, s % KT
                    g, half = hs // HALVES, hs % HALVES
                    n_half = HALF_STEPS * b + hs
                    if kt == 0 and has_maxima(hs, last):
                        dve.wait_ge(max_turned, n_half + 1)
                    for j in range(2):
                        if has_maxima(hs, last):
                            unit = 2 * kt + j
                            reduce_max(half, unit, UNITS * (n_half + HALVES) + unit, at)
                            at += 1
                        if j == 0:
                            for name in turns(hs, kt, first, last):
                                if name == "max":
                                    turn_use = base + at
                                    split_max(1 - half, n_half + 1, GROUPS * b + g + half, turn_use, at)
                                elif name == "outputs" and hs:
                                    normalise(hs - 1, n_half - 1, base + at, at)
                                else:
                                    end_of_batch(name, b if hs > 1 else b - 1, base + at, at)
                                at += 1
                        if "max" in turns(hs, kt, first, last) and j == 1:
                            mid_of_max(1 - half, turn_use)
                        if "max" in turns(hs, kt - 1, first, last) and j == 0:
                            low_of_max(1 - half, n_half + 1)
                return base, at

            for half in range(HALVES):
                for unit in range(UNITS):
                    reduce_max(half, unit, half * UNITS + unit, half * UNITS + unit)
            split_max(0, 0, 0, HALVES * UNITS, HALVES * UNITS)
            mid_of_max(0, HALVES * UNITS)
            low_of_max(0, 0)
            batch(0, True, False)
            with dve.Fori(1, batches - 1) as b:
                batch(b, False, False)
            base, at = batch(batches - 1, False, True)
            for name in END:
                end_of_batch(name, batches - 1, base + at, at)
                at += 1

        @block.gpsimd
        def _(pool):
            pool.sem_inc(summed, summed0)

            def add_x(hq, use):
                pool.wait_ge(ring_free, use + 1 + ring0)
                tiles = slice(hq * QT, (hq + 1) * QT)
                nc.gpsimd.tensor_tensor(y_b[:, tiles], y_b[:, tiles], x_b[:, tiles], ALU.add).then_inc(summed, 1)

            def batch(b, last):
                base, at = ring_start(b, False)
                for hq in range(2):
                    add_x(hq, base + at + ring_use(False, last, f"project{hq}"))

            with pool.Fori(1, batches - 1) as b:
                batch(b, False)
            batch(batches - 1, True)
            base, at = ring_start(batches - 1, False)
            add_x(0, base + at + ring_use(False, True, "project0", HALF_STEPS - 1))
            add_x(1, base + at + ring_use(False, True) + END.index("project1"))


def build(nc, x, w_q, w_k, w_v, w_o, w_gate_t, w_up_t, w_down_t, out):
    batches, seq, dim = x.shape
    tokens = batches * seq
    q_parts = nc.dram_tensor("q_parts", (3, HEADS * HEAD_DIM, tokens), BF16).ap()
    k_parts = nc.dram_tensor("k_parts", (3, GROUPS * HEAD_DIM, tokens), BF16).ap()
    v_rows = nc.dram_tensor("v_rows", (tokens, GROUPS * HEAD_DIM), F32).ap()
    gate_rows = nc.dram_tensor("gate_rows", (tokens, dim), F32).ap()
    x_rows = x.rearrange("b t d -> (b t) d")
    out_rows = out.rearrange("b t d -> (b t) d")
    with ExitStack() as ctx:
        psum = ctx.enter_context(nc.psum_tensor("psum", [P, 8, BANK], F32))
        ident = ctx.enter_context(nc.sbuf_tensor("ident", [P, P], F32))
        ident_step = ctx.enter_context(nc.semaphore("ident_step"))
        with nc.Block() as block:
            @block.gpsimd
            def _(pool):
                nc.gpsimd.memset(ident[:], 0.0).then_inc(ident_step, 1)
                pool.wait_ge(ident_step, 1)
                nc.gpsimd.affine_select(out=ident[:], in_=ident[:], compare_op=ALU.not_equal, fill=1.0, base=0,
                                        pattern=[[-1, P]], channel_multiplier=1).then_inc(ident_step, 1)
                pool.wait_ge(ident_step, 2)
        project(nc, psum, ident, x_rows, w_q, w_k, w_v, w_gate_t, w_up_t, w_down_t,
                q_parts, k_parts, v_rows, gate_rows)
        attend(nc, psum, ident, x_rows, w_o, q_parts, k_parts, v_rows, gate_rows, out_rows, batches)


def kernel(**inputs):
    import numpy as np
    from concourse import bacc
    from concourse.bass_utils import run_bass_kernel_spmd

    nc = bacc.Bacc("TRN2", target_bir_lowering=False, num_devices=1)
    arrays = {
        "x": inputs["L0_attn_x"], "w_q": inputs["L0_attn_Wq"], "w_k": inputs["L0_attn_Wk"],
        "w_v": inputs["L0_attn_Wv"], "w_o": inputs["L0_attn_Wo"],
        "w_gate_t": np.transpose(inputs["L0_ffn_w_gate"]), "w_up_t": np.transpose(inputs["L0_ffn_w_up"]),
        "w_down_t": np.transpose(inputs["L0_ffn_w_down"]),
    }
    arrays = {name: np.ascontiguousarray(a) for name, a in arrays.items()}
    args = [nc.dram_tensor(name, a.shape, mybir.dt.from_np(a.dtype), kind="ExternalInput").ap()
            for name, a in arrays.items()]
    out = nc.dram_tensor("out", arrays["x"].shape, F32, kind="ExternalOutput").ap()
    build(nc, *args, out)
    r = run_bass_kernel_spmd(nc, [arrays], core_ids=[0])
    return r.results[0]["out"]
```

```python
from contextlib import ExitStack

import concourse.bass as bass
from concourse import mybir

ALU = mybir.AluOpType
ACT = mybir.ActivationFunctionType
AX = mybir.AxisListType
F32 = mybir.dt.float32
BF16 = mybir.dt.bfloat16
F16 = mybir.dt.float16
I32 = mybir.dt.int32

P = 128
BANK = 512
HEADS, GROUPS, HEAD_DIM = 16, 4, 16
PER_GROUP = HEADS // GROUPS
EPS = 1e-5
WEIGHT_SCALE = 1.0 / 127.0
SCORE_SCALE = HEAD_DIM ** -0.5

TERMS = [(0, 0), (0, 1), (0, 2), (1, 0), (1, 1), (2, 0)]
STACK = len(TERMS) * HEAD_DIM
ROWS = STACK + 3


class Maxima:
    RING_BANK = 4
    RING0 = 2
    MAX_IN0 = 16

    def __init__(self, nc, ctx, psum, ident, q_parts, k_parts, v_in, seq):
        self.nc, self.psum, self.ident = nc, psum, ident
        self.KT = KT = seq // P
        self.HALVES = HALVES = seq // BANK
        self.QT = BANK // P
        self.UNITS = UNITS = PER_GROUP * self.QT
        self.LOADS = (HALVES + 1) * len(TERMS) + 1
        self.FIRST_TURN = UNITS + 2
        self.FIRST_USES = HALVES * UNITS + 1
        self.q_v = q_parts.rearrange("a (g j d) (b n) -> a b g d j n", g=GROUPS, d=HEAD_DIM, n=seq)
        self.k_v = k_parts.rearrange("a (g d) (b n) -> a b g d n", g=GROUPS, n=seq)
        self.v_v = v_in.rearrange("(b t p) (g d) -> b g p t d", t=KT, p=P, g=GROUPS)

        def sb(name, shape, dt=F32):
            return ctx.enter_context(nc.sbuf_tensor(name, shape, dt))

        def sem(name):
            return ctx.enter_context(nc.semaphore(name))

        self.q_stack = sb("q_stack", [P, GROUPS, HALVES, PER_GROUP * BANK], BF16)
        self.k_stack = sb("k_stack", [P, GROUPS, seq], BF16)
        self.v_ones = sb("v_ones", [P, GROUPS, KT, 2 * HEAD_DIM])
        self.minus_max = sb("minus_max", [P, HALVES, UNITS])
        self.max_rest = sb("max_rest", [UNITS, HALVES, P])
        self.max_parts = sb("max_parts", [UNITS, HALVES, 3, P], BF16)

        self.ones_done = sem("ones_done")
        self.loaded = [sem(f"loaded{g}") for g in range(GROUPS)]
        self.max_in = [sem("max_in0"), sem("max_in1")]
        self.max_scores_done = sem("max_scores_done")
        self.max_turned = sem("max_turned")
        self.split_chain = sem("split_chain")
        self.max_split = sem("max_split")
        self.ring_free = sem("ring_free")

    def ring_bank(self, at):
        return self.RING_BANK + 2 * (at % 2)

    def first_uses(self, start=0, end=None):
        for use in range(start, self.FIRST_USES if end is None else end):
            yield use, None if use == self.FIRST_TURN else use - (use > self.FIRST_TURN)


    def load_step(self, sp, b, g):
        q_stack, k_stack, loaded = self.q_stack, self.k_stack, self.loaded[g]
        for t, (a, c) in enumerate(TERMS):
            rows = slice(t * HEAD_DIM, (t + 1) * HEAD_DIM)
            for half in range(self.HALVES):
                sp.dma_start(q_stack[rows, g, half].rearrange("d (j n) -> d j n", n=BANK),
                             self.q_v[a, b, g, :, :, half * BANK:(half + 1) * BANK]).then_inc(loaded, 16)
            sp.dma_start(k_stack[rows, g], self.k_v[c, b, g]).then_inc(loaded, 16)
        sp.dma_start(self.v_ones[:, g, :, 0:HEAD_DIM], self.v_v[b, g]).then_inc(loaded, 16)

    def send_max(self, sp, half, g, n):
        sp.wait_ge(self.max_split, n + 1)
        for a in range(3):
            sp.dma_start(self.q_stack[STACK + a:STACK + a + 1, g, half],
                         self.max_parts[:, half, a]).then_inc(self.max_in[half], 16)


    def max_scores(self, pe, g, half, unit, use, at):
        j, qt = unit // self.QT, unit % self.QT
        q0 = j * BANK + qt * P
        pe.wait_ge(self.ring_free, use - 1 + self.RING0)
        for kh in range(self.HALVES):
            ins = pe.matmul(self.psum[:, self.ring_bank(at) + kh], self.q_stack[0:STACK, g, half, q0:q0 + P],
                            self.k_stack[0:STACK, g, kh * BANK:(kh + 1) * BANK], start=True, stop=True)
        ins.then_inc(self.max_scores_done, 1)

    def turn_max(self, pe, half, use, at, settled):
        pe.wait_ge(self.ring_free, use - (0 if settled else 1) + self.RING0)
        pe.transpose(self.psum[0:self.UNITS, self.ring_bank(at), 0:P], self.minus_max[:, 1 - half],
                     self.ident[:]).then_inc(self.max_turned, 1)

    def first_scores(self, pe, start, end=None):
        for use, unit in self.first_uses(start, end):
            if unit is None:
                self.turn_max(pe, 1, use, use, False)
            else:
                self.max_scores(pe, 0, unit // self.UNITS, unit % self.UNITS, use, use)


    def set_ones(self, dve, g):
        self.nc.vector.memset(self.k_stack[STACK:ROWS, g], 1.0).then_inc(self.ones_done, 1)
        self.nc.vector.memset(self.v_ones[:, g, :, HEAD_DIM:], 1.0).then_inc(self.ones_done, 1)

    def reduce_max(self, dve, half, unit, n, at):
        dve.wait_ge(self.max_scores_done, n + 1)
        bank = self.ring_bank(at)
        self.nc.vector.tensor_reduce(self.minus_max[:, half, unit:unit + 1],
                                     self.psum[:, bank:bank + 2].rearrange("p a n -> p (a n)"), AX.X, ALU.max,
                                     negate=True).then_inc(self.ring_free, 1)

    def split_max(self, dve, half, n, sent, use, at):
        dve.wait_ge(self.max_turned, n + 1)
        dve.wait_ge(self.max_in[half], 3 * 16 * sent + self.MAX_IN0)
        turned = self.psum[0:self.UNITS, self.ring_bank(at), 0:P]
        self.nc.vector.tensor_copy(self.max_parts[:, half, 0], turned).then_inc(self.split_chain, 1)
        dve.wait_ge(self.split_chain, 2 * n + 1)
        self.nc.vector.tensor_tensor(self.max_rest[:, half], turned, self.max_parts[:, half, 0],
                                     ALU.subtract).then_inc(self.ring_free, 1)

    def mid_of_max(self, dve, half, use):
        dve.wait_ge(self.ring_free, use + 1 + self.RING0)
        self.nc.vector.tensor_copy(self.max_parts[:, half, 1], self.max_rest[:, half]).then_inc(self.split_chain, 1)

    def low_of_max(self, dve, half, n):
        dve.wait_ge(self.split_chain, 2 * n + 2)
        self.nc.vector.tensor_tensor(self.max_parts[:, half, 2], self.max_rest[:, half], self.max_parts[:, half, 1],
                                     ALU.subtract).then_inc(self.max_split, 1)

    def first_reductions(self, dve):
        for use, unit in self.first_uses():
            if unit is None:
                self.split_max(dve, 0, 0, 0, use, use)
                self.mid_of_max(dve, 0, use)
                self.low_of_max(dve, 0, 0)
            else:
                self.reduce_max(dve, unit // self.UNITS, unit % self.UNITS, unit, use)


def project(nc, psum, ident, maxima, x, w_q, w_k, w_v, w_gate_t, w_up_t, w_down_t, q_parts, k_parts, v_out, gate_out):
    tokens, dim = x.shape
    hidden = w_gate_t.shape[1]
    T = BANK // P
    CHUNKS = tokens // BANK
    KD = dim // P
    KH = hidden // P
    KV = GROUPS * HEAD_DIM
    PROJ = [(2, BANK), (3, BANK), (0, BANK // 2)]
    HALF = BANK // 2
    V_BANK = 1
    TURN = KH - 2
    EXACT = 128
    XN_SCALE = 2.0 ** 8
    H_SCALE = 2.0 ** -8
    assert (dim * EXACT) * WEIGHT_SCALE * (dim * EXACT) * H_SCALE < 65504
    assert dim ** 0.5 * XN_SCALE < 65504
    assert 2 * KV == P and KD == 2 and CHUNKS % 2 == 0 and CHUNKS >= 4 and T * KV <= BANK

    x_v = x.rearrange("(c t p) d -> c p t d", t=T, p=P)
    gate_v = gate_out.rearrange("(c t p) d -> c p t d", t=T, p=P)
    v_v = v_out.rearrange("(c t p) d -> c p t d", t=T, p=P)
    q_v = q_parts.rearrange("a (r p) (c n) -> c r p a n", p=P, n=BANK)
    k_v = k_parts.rearrange("a p (c s n) -> c s p a n", s=2, n=BANK // 2)

    with ExitStack() as ctx:
        def sb(name, shape, dt=F32):
            return ctx.enter_context(nc.sbuf_tensor(name, shape, dt))

        def sem(name):
            return ctx.enter_context(nc.semaphore(name))

        wq = sb("wq", [P, KD, dim])
        wk = sb("wk", [P, KD, KV])
        wv = sb("wv", [P, KD, KV])
        w_int = sb("w_int", [P, 3, KD * hidden], I32)
        w_full = sb("w_full", [P, 3, KD * hidden])
        w_half = sb("w_half", [P, 3, KD * hidden], F16)
        w_largest = sb("w_largest", [P, 1])
        w_largest_all = sb("w_largest_all", [1, 1])
        w_large = sb("w_large", [1, 1], I32)
        x_t = sb("x_t", [P, 2, T, dim])
        stats = sb("stats", [P, T, 6])
        moments = sb("moments", [P, T, 2])
        var_eps = sb("var_eps", [P, T])
        minus_half = sb("minus_half", [P, T])
        eps = sb("eps", [P, T])
        pause = sb("pause", [P, 1])
        rsqrt = sb("rsqrt", [P, T])
        rstd = sb("rstd", [P, T])
        xn_scale = sb("xn_scale", [P, T])
        xn = sb("xn", [P, T, dim])
        xn_t = sb("xn_t", [P, 2, KD, BANK])
        xn_high = sb("xn_high", [P, 2, KD, BANK], F16)
        xn_low = sb("xn_low", [P, 2, KD, BANK], F16)
        parts = sb("parts", [P, 3, 3, BANK], BF16)
        rest = sb("rest", [P, 3, BANK])
        v_free = sb("v_free", [P, HALF])
        v_t = sb("v_t", [P, T, KV])
        silu_gate = sb("silu_gate", [P, 2, BANK])
        h_t = sb("h_t", [P, KH, BANK])
        h_high = sb("h_high", [P, KH, BANK], F16)
        h_low = sb("h_low", [P, KH, BANK], F16)
        gate_t = sb("gate_t", [P, T, dim])

        def views(w):
            return (w[:, 0].rearrange("p (k n) -> p k n", k=KD), w[:, 1].rearrange("p (k n) -> p k n", k=KD),
                    w[:, 2].rearrange("p (k n) -> p k n", k=KH))

        proj_weights_in = sem("proj_weights_in")
        proj_weights_scaled = sem("proj_weights_scaled")
        ffn_weights_in = sem("ffn_weights_in")
        weights_ready = sem("weights_ready")
        largest_done = sem("largest_done")
        largest_turned = sem("largest_turned")
        large_known = sem("large_known")
        consts_ready = sem("consts_ready")
        x_in = [sem("x_in_even"), sem("x_in_odd")]
        stats_chain = sem("stats_chain")
        stats_done = sem("stats_done")
        var_done = sem("var_done")
        rsqrt_done = sem("rsqrt_done")
        rstd_done = sem("rstd_done")
        xn_done = sem("xn_done")
        turned = sem("turned")
        xn_t_done = sem("xn_t_done")
        xn_low_done = sem("xn_low_done")
        proj_done = sem("proj_done")
        high_done = sem("high_done")
        rest_done = sem("rest_done")
        mid_done = sem("mid_done")
        low_done = sem("low_done")
        v_copied = sem("v_copied")
        v_turned = sem("v_turned")
        v_done = sem("v_done")
        gate_up_done = sem("gate_up_done")
        silu_done = sem("silu_done")
        h_done = sem("h_done")
        h_high_done = sem("h_high_done")
        h_low_done = sem("h_low_done")
        down_done = sem("down_done")
        gate_done = sem("gate_done")
        qk_stored = sem("qk_stored")
        v_stored = sem("v_stored")
        gate_stored = sem("gate_stored")
        QK_STORES = 4 * 16

        turned0, xn_t0, v0, gate0, gate_up0, h0, h_low0, rest0, low0, down0 = 1, 1, 1, 4, 2 * KH, 2, 1, 1, 3, 1
        stored0 = 16

        block = ctx.enter_context(nc.Block())

        def pairs(engine, pair):
            with engine.Fori(0, CHUNKS // 2 - 1) as i:
                pair(i, False)
            pair(CHUNKS // 2 - 1, True)

        @block.sync
        def _(sp):
            sp.sem_inc(qk_stored, stored0)
            sp.sem_inc(v_stored, stored0)
            sp.sem_inc(gate_stored, stored0)
            for half in range(maxima.HALVES):
                sp.sem_inc(maxima.max_in[half], maxima.MAX_IN0)

            def store_projections(n):
                for r in range(3):
                    sp.wait_ge(low_done, 3 * n + r + 1 + low0)
                    if r < 2:
                        sp.dma_start(q_v[n, r], parts[:, r]).then_inc(qk_stored, 16)
                    else:
                        for s in range(2):
                            sp.dma_start(k_v[n, s], parts[s * KV:(s + 1) * KV, r, :, 0:BANK // 2]).then_inc(qk_stored, 16)
                sp.wait_ge(v_done, n + 1 + v0)
                sp.dma_start(v_v[n], v_t[:]).then_inc(v_stored, 16)

            def pair(i, last):
                for sub in range(2):
                    c = 2 * i + sub
                    if not last:
                        sp.wait_ge(xn_done, c + 1)
                        sp.dma_start(x_t[:, sub], x_v[c + 2]).then_inc(x_in[sub], 16)
                    if last and sub == 0:
                        sp.wait_ge(qk_stored, QK_STORES * (CHUNKS - 1) + stored0)
                        sp.wait_ge(v_stored, 16 * (CHUNKS - 1) + stored0)
                        for g in range(GROUPS - 1):
                            maxima.load_step(sp, 0, g)
                    if not (last and sub == 1):
                        store_projections(c + 1)
                    sp.wait_ge(gate_done, 2 * c + 2 + gate0)
                    sp.dma_start(gate_v[c], gate_t[:]).then_inc(gate_stored, 16)

            sp.dma_start(x_t[:, 0], x_v[0]).then_inc(x_in[0], 16)
            sp.dma_start(wq[:], w_q.rearrange("(k p) n -> p k n", p=P)).then_inc(proj_weights_in, 16)
            sp.dma_start(wk[:], w_k.rearrange("(k p) n -> p k n", p=P)).then_inc(proj_weights_in, 16)
            sp.dma_start(wv[:], w_v.rearrange("(k p) n -> p k n", p=P)).then_inc(proj_weights_in, 16)
            for dst, w in zip(views(w_int), (w_gate_t, w_up_t, w_down_t)):
                sp.dma_start(dst, w.rearrange("(k p) n -> p k n", p=P)).then_inc(ffn_weights_in, 16)
            sp.dma_start(x_t[:, 1], x_v[1]).then_inc(x_in[1], 16)
            store_projections(0)
            pairs(sp, pair)
            maxima.send_max(sp, 0, 0, 0)
            sp.wait_ge(qk_stored, QK_STORES * CHUNKS + stored0)
            sp.wait_ge(v_stored, 16 * CHUNKS + stored0)
            sp.wait_ge(gate_stored, 16 * CHUNKS + stored0)

        @block.vector
        def _(dve):
            dve.sem_inc(h_done, h0)
            dve.sem_inc(rest_done, rest0)
            dve.sem_inc(maxima.ring_free, maxima.RING0)
            nc.vector.memset(minus_half[:], -0.5).then_inc(consts_ready, 1)
            nc.vector.memset(eps[:], EPS).then_inc(consts_ready, 1)
            nc.vector.memset(xn_scale[:], XN_SCALE).then_inc(consts_ready, 1)

            def normalise(n, lap, sub):
                dve.wait_ge(x_in[sub], 16 * lap + 16)
                for t in range(T):
                    ins = nc.vector.bn_stats(stats[:, t], x_t[:, sub, t])
                ins.then_inc(stats_chain, 1)
                dve.wait_ge(stats_chain, n + 1)
                nc.vector.memset(pause[:], 0.0)
                for t in range(T):
                    ins = nc.vector.bn_aggr(moments[:, t], stats[:, t])
                ins.then_inc(stats_done, 1)
                dve.wait_ge(rstd_done, n + 1)
                dve.wait_ge(turned, 2 * n + turned0)
                for t in range(T):
                    ins = nc.vector.tensor_scalar(xn[:, t], x_t[:, sub, t], moments[:, t, 0:1], rstd[:, t:t + 1],
                                                  ALU.subtract, ALU.mult)
                ins.then_inc(xn_done, 1)

            def split_projections(n):
                for r, (bank, w) in enumerate(PROJ):
                    dve.wait_ge(high_done, 3 * n + r + 1)
                    dve.wait_ge(low_done, 3 * (n - 1) + r + 1 + low0)
                    nc.vector.tensor_tensor(rest[:, r, 0:w], psum[:, bank, 0:w], parts[:, r, 0, 0:w],
                                            ALU.subtract).then_inc(rest_done, 1)
                    dve.wait_ge(rest_done, 3 * n + r + 1 + rest0)
                    nc.vector.tensor_copy(parts[:, r, 1, 0:w], rest[:, r, 0:w]).then_inc(mid_done, 1)

            def hidden_values(c, m):
                dve.wait_ge(silu_done, KH * c + m + 1)
                if m == 0:
                    dve.wait_ge(h_low_done, KH * c + h_low0)
                    dve.wait_ge(down_done, 2 * c + down0)
                nc.vector.scalar_tensor_tensor(h_t[:, m], psum[:, 5 + 2 * (m % 2)], H_SCALE / XN_SCALE, silu_gate[:, m % 2],
                                               ALU.mult, ALU.mult).then_inc(h_done, 1)
                dve.wait_ge(h_done, KH * c + m + 1 + h0)
                nc.vector.tensor_copy(h_high[:, m], h_t[:, m]).then_inc(h_high_done, 1)

            def pair(i, last):
                for sub in range(2):
                    c, ahead = 2 * i + sub, not (last and sub == 1)
                    if ahead:
                        normalise(c + 1, i + sub, 1 - sub)
                    for m in range(KH):
                        hidden_values(c, m)
                        if last and sub == 0 and m < GROUPS:
                            maxima.set_ones(dve, m)
                    if ahead:
                        split_projections(c + 1)

            normalise(0, 0, 0)
            dve.wait_ge(proj_weights_in, 3 * 16)
            for w in (wq, wk, wv):
                nc.vector.tensor_scalar(w[:], w[:], 1.0 / XN_SCALE, None, ALU.mult).then_inc(proj_weights_scaled, 1)
            dve.wait_ge(ffn_weights_in, 3 * 16)
            nc.vector.tensor_reduce(w_largest[:], w_int[:].rearrange("p w n -> p (w n)"), AX.X, ALU.max,
                                    apply_absolute_value=True).then_inc(largest_done, 1)
            nc.vector.tensor_copy(w_full[:], w_int[:]).then_inc(weights_ready, 1)
            dve.wait_ge(weights_ready, 1)
            nc.vector.tensor_copy(w_half[:], w_full[:]).then_inc(weights_ready, 1)
            split_projections(0)
            dve.wait_ge(largest_turned, 1)
            nc.vector.tensor_reduce(w_largest_all[:], psum[0:1, 7, 0:P], AX.X, ALU.max).then_inc(largest_done, 1)
            dve.wait_ge(largest_done, 2)
            nc.vector.tensor_scalar(w_large[:], w_largest_all[:], float(EXACT), None,
                                    ALU.is_gt).then_inc(large_known, 1)
            pairs(dve, pair)
            maxima.first_reductions(dve)

        @block.gpsimd
        def _(pool):
            pool.sem_inc(low_done, low0)
            pool.sem_inc(h_low_done, h_low0)

            def rstd_of(n):
                pool.wait_ge(stats_done, n + 1)
                nc.gpsimd.tensor_tensor(var_eps[:], moments[:, :, 1], eps[:], ALU.add).then_inc(var_done, 1)
                pool.wait_ge(var_done, n + 1)
                nc.gpsimd.tensor_tensor(rsqrt[:], var_eps[:], minus_half[:], ALU.pow).then_inc(rsqrt_done, 1)
                pool.wait_ge(rsqrt_done, n + 1)
                nc.gpsimd.tensor_tensor(rstd[:], rsqrt[:], xn_scale[:], ALU.mult).then_inc(rstd_done, 1)

            def low_of_xn(n, sub):
                for k in range(KD):
                    pool.wait_ge(xn_t_done, 2 * KD * n + KD + k + 1 + xn_t0)
                    nc.gpsimd.tensor_tensor(xn_low[:, sub, k], xn_t[:, sub, k], xn_high[:, sub, k],
                                            ALU.subtract).then_inc(xn_low_done, 1)

            def low_of_projections(n):
                for r, (_, w) in enumerate(PROJ):
                    pool.wait_ge(mid_done, 3 * n + r + 1)
                    nc.gpsimd.tensor_tensor(parts[:, r, 2, 0:w], rest[:, r, 0:w], parts[:, r, 1, 0:w],
                                            ALU.subtract).then_inc(low_done, 1)

            def low_of_hidden(c, m):
                pool.wait_ge(h_high_done, KH * c + m + 1)
                nc.gpsimd.tensor_tensor(h_low[:, m], h_t[:, m], h_high[:, m], ALU.subtract).then_inc(h_low_done, 1)

            def pair(i, last):
                for sub in range(2):
                    c, ahead = 2 * i + sub, not (last and sub == 1)
                    if ahead:
                        rstd_of(c + 1)
                    for m in range(KH - 1):
                        low_of_hidden(c, m)
                    if ahead:
                        low_of_xn(c + 1, 1 - sub)
                    low_of_hidden(c, KH - 1)
                    if ahead:
                        low_of_projections(c + 1)

            pool.wait_ge(consts_ready, 3)
            rstd_of(0)
            low_of_xn(0, 0)
            low_of_projections(0)
            pairs(pool, pair)

        @block.tensor
        def _(pe):
            pe.sem_inc(turned, turned0)
            pe.sem_inc(gate_up_done, gate_up0)
            pe.sem_inc(down_done, down0)

            def turn_xn(n):
                pe.wait_ge(xn_done, n + 1)
                pe.wait_ge(rest_done, 3 * n + rest0)
                pe.wait_ge(v_done, n + v0)
                for k in range(KD):
                    for t in range(T):
                        ins = pe.transpose(psum[:, k, t * P:(t + 1) * P], xn[:, t, k * P:(k + 1) * P], ident[:])
                    ins.then_inc(turned, 1)

            def project_chunk(n, sub):
                pe.wait_ge(xn_t_done, 2 * KD * n + KD + xn_t0)
                for r in range(2):
                    bank = PROJ[r][0]
                    pe.wait_ge(gate_done, 2 * (n - 2) + r + 1 + gate0)
                    for k in range(KD):
                        ins = pe.matmul(psum[:, bank], wq[:, k, r * P:(r + 1) * P], xn_t[:, sub, k],
                                        start=(k == 0), stop=(k == KD - 1))
                    ins.then_inc(proj_done, 1)
                pe.wait_ge(xn_t_done, 2 * KD * (n + 1) + xn_t0)
                for w, bank in ((wk, PROJ[2][0]), (wv, V_BANK)):
                    for k in range(KD):
                        for s in range(2):
                            ins = pe.matmul(psum[s * KV:(s + 1) * KV, bank, 0:HALF], w[:, k],
                                            xn_t[:, sub, k, s * HALF:(s + 1) * HALF],
                                            start=(k == 0), stop=(k == KD - 1))
                    ins.then_inc(proj_done, 1)

            def turn_v(n):
                pe.wait_ge(v_copied, n + 1)
                for t in range(T // 2):
                    ins = pe.transpose(psum[:, V_BANK, HALF + t * P:HALF + (t + 1) * P], v_free[:, t * P:(t + 1) * P],
                                       ident[:])
                ins.then_inc(v_turned, 1)

            def accumulate(out, products):
                for n, (lhs, rhs) in enumerate(products):
                    ins = pe.matmul(out, lhs, rhs, start=(n == 0), stop=(n == len(products) - 1))
                return ins

            def gate_up(c, m, sub, large):
                pe.wait_ge(h_done, KH * c + m - 1 + h0)
                hid = slice(m * P, (m + 1) * P)
                for w in range(2):
                    if large:
                        products = [(views(w_full)[w][:, k, hid], xn_t[:, sub, k]) for k in range(KD)]
                    else:
                        products = [(views(w_half)[w][:, k, hid], part[:, sub, k])
                                    for k in range(KD) for part in (xn_high, xn_low)]
                    ins = accumulate(psum[:, 4 + 2 * (m % 2) + w], products)
                ins.then_inc(gate_up_done, 1)

            def down(c, ahead, large):
                if not ahead:
                    pe.wait_ge(maxima.loaded[0], 16 * maxima.LOADS)
                    for use in range(2):
                        pe.wait_ge(h_done, KH * (c + 1) - 1 + use + h0)
                        maxima.first_scores(pe, use, use + 1)
                pe.wait_ge(h_low_done, KH * (c + 1) + h_low0)
                for t in range(T):
                    if t == T // 2 and ahead:
                        turn_v(c + 1)
                    if t % 2 == 0:
                        pe.wait_ge(rest_done, 3 * (c + ahead) + t // 2 + 1 + rest0)
                    tok = slice(t * P, (t + 1) * P)
                    if large:
                        products = [(h_t[:, m, tok], views(w_full)[2][:, m]) for m in range(KH)]
                    else:
                        products = [(part[:, m, tok], views(w_half)[2][:, m])
                                    for m in range(KH) for part in (h_high, h_low)]
                    ins = accumulate(psum[:, 2 + t // 2, (t % 2) * dim:(t % 2 + 1) * dim], products)
                    if t % 2 == 1:
                        ins.then_inc(down_done, 1)
                    if not ahead:
                        maxima.first_scores(pe, t + 2, t + 3)

            def chunks(large):
                def pair(i, last):
                    for sub in range(2):
                        c, ahead = 2 * i + sub, not (last and sub == 1)
                        pe.wait_ge(xn_low_done, KD * (c + 1))
                        for m in range(KH):
                            if m == TURN and ahead:
                                turn_xn(c + 1)
                            gate_up(c, m, sub, large)
                        if ahead:
                            project_chunk(c + 1, 1 - sub)
                        down(c, ahead, large)
                pairs(pe, pair)

            turn_xn(0)
            pe.wait_ge(proj_weights_scaled, 3)
            project_chunk(0, 0)
            turn_v(0)
            pe.wait_ge(largest_done, 1)
            pe.transpose(psum[0:1, 7, 0:P], w_largest[:], ident[:]).then_inc(largest_turned, 1)
            pe.wait_ge(weights_ready, 2)
            pe.wait_ge(large_known, 1)
            large = pe.value_load(w_large[0:1, 0:1])
            with pe.If(large > 0):
                chunks(True)
            with pe.Else():
                chunks(False)
            maxima.first_scores(pe, T + 2)

        @block.scalar
        def _(act):
            act.sem_inc(xn_t_done, xn_t0)
            act.sem_inc(v_done, v0)
            act.sem_inc(gate_done, gate0)
            act.preload_act_table(ACT.Silu)

            def copy_xn(n, sub):
                act.wait_ge(gate_up_done, KH * (n - 1) + gate_up0)
                for k in range(KD):
                    act.wait_ge(turned, 2 * n + k + 1 + turned0)
                    nc.scalar.copy(xn_t[:, sub, k], psum[:, k]).then_inc(xn_t_done, 1)
                for k in range(KD):
                    nc.scalar.copy(xn_high[:, sub, k], psum[:, k]).then_inc(xn_t_done, 1)

            def copy_projections(n):
                act.wait_ge(qk_stored, QK_STORES * n + stored0)
                for r, (bank, w) in enumerate(PROJ):
                    act.wait_ge(proj_done, 4 * n + r + 1)
                    nc.scalar.copy(parts[:, r, 0, 0:w], psum[:, bank, 0:w]).then_inc(high_done, 1)
                act.wait_ge(proj_done, 4 * n + 4)
                nc.scalar.copy(v_free[:], psum[:, V_BANK, 0:HALF]).then_inc(v_copied, 1)

            def copy_v(n):
                act.wait_ge(v_turned, n + 1)
                act.wait_ge(v_stored, 16 * n + stored0)
                nc.scalar.copy(v_t[:].rearrange("p (s t) n -> p t s n", s=2),
                               psum[:, V_BANK, HALF:].rearrange("p (t s n) -> p t s n", s=2, n=KV)).then_inc(v_done, 1)

            def silu_of_gate(c, m):
                act.wait_ge(gate_up_done, KH * c + m + 1 + gate_up0)
                act.wait_ge(h_done, KH * c + m - 1 + h0)
                nc.scalar.activation(silu_gate[:, m % 2], psum[:, 4 + 2 * (m % 2)], ACT.Silu,
                                     scale=WEIGHT_SCALE / XN_SCALE).then_inc(silu_done, 1)

            def pair(i, last):
                for sub in range(2):
                    c, ahead = 2 * i + sub, not (last and sub == 1)
                    for m in range(KH):
                        if m == TURN and ahead:
                            copy_xn(c + 1, 1 - sub)
                        silu_of_gate(c, m)
                    if ahead:
                        copy_projections(c + 1)
                    act.wait_ge(gate_stored, 16 * c + stored0)
                    for n in range(2):
                        if n == 1 and ahead:
                            copy_v(c + 1)
                        act.wait_ge(down_done, 2 * c + n + 1 + down0)
                        nc.scalar.activation(gate_t[:, 2 * n:2 * n + 2].rearrange("p t d -> p (t d)"),
                                             psum[:, 2 + n], ACT.Silu,
                                             scale=WEIGHT_SCALE * WEIGHT_SCALE / H_SCALE).then_inc(gate_done, 1)

            copy_xn(0, 0)
            copy_projections(0)
            copy_v(0)
            pairs(act, pair)
            act.preload_act_table(ACT.Exp)


def attend(nc, psum, ident, maxima, x, w_o, gate_in, out, batches):
    tokens, dim = x.shape
    KT, HALVES, QT, UNITS = maxima.KT, maxima.HALVES, maxima.QT, maxima.UNITS
    RING_PROLOGUE, ring_bank, ring0 = maxima.FIRST_USES, maxima.ring_bank, maxima.RING0
    seq = tokens // batches
    HALF_STEPS = GROUPS * HALVES
    SLOTS = HALF_STEPS * KT
    S_BANKS, O_BANK = 3, 3
    LAG = 2
    NR = 4
    assert HALVES == 2 and PER_GROUP == 4 and KT == 2 * QT and dim == 2 * P and batches >= 3

    x_v = x.rearrange("(b t p) d -> b p t d", t=KT, p=P)
    gate_v = gate_in.rearrange("(b t p) d -> b p t d", t=KT, p=P)
    out_v = out.rearrange("(b t p) d -> b p t d", t=KT, p=P)
    END = ("outputs", "norm1", "project1")

    def turns(hs, kt, first, last):
        found = []
        if kt == 2 and not (last and hs == HALF_STEPS - 1):
            found.append("max")
        if kt == 5 and not (first and hs == 0):
            found.append("outputs")
        if hs == 1 and not first:
            found += {1: ["norm0"], 3: ["norm1"], 4: ["project0"], 6: ["project1"]}.get(kt, [])
        if last and hs == HALF_STEPS - 1:
            found += {6: ["norm0"], 7: ["project0"]}.get(kt, [])
        return found

    def has_maxima(hs, last):
        return not (last and hs // HALVES == GROUPS - 1)

    def ring_use(first, last, name=None, since=0):
        n = 0
        for hs in range(HALF_STEPS):
            for kt in range(KT):
                n += has_maxima(hs, last)
                for turn in turns(hs, kt, first, last):
                    if turn == name and hs >= since:
                        return n
                    n += 1
                n += has_maxima(hs, last)
        return n

    RING_FIRST = ring_use(True, False)
    RING_BATCH = ring_use(False, False)
    assert RING_BATCH % 2 == 0

    def ring_start(b, first):
        return (0, RING_PROLOGUE) if first else (RING_BATCH * (b - 1), RING_PROLOGUE + RING_FIRST)

    with ExitStack() as ctx:
        def sb(name, shape, dt=F32):
            return ctx.enter_context(nc.sbuf_tensor(name, shape, dt))

        def sem(name):
            return ctx.enter_context(nc.semaphore(name))

        wo = sb("wo", [P, 2, dim])
        probs = sb("probs", [P, NR, PER_GROUP, BANK])
        o_sum = sb("o_sum", [P, BANK])
        inv_sum = sb("inv_sum", [P, QT, PER_GROUP])
        o_norm = sb("o_norm", [P, KT, dim])
        o_norm_t = sb("o_norm_t", [P, 2, seq])
        x_b = sb("x_b", [P, KT, dim])
        gate_b = sb("gate_b", [P, KT, dim])
        y_b = sb("y_b", [P, KT, dim])

        wo_in = sem("wo_in")
        residual_in = sem("residual_in")
        scores_done = sem("scores_done")
        exp_done = sem("exp_done")
        av_done = sem("av_done")
        o_copied = sem("o_copied")
        o_turned = sem("o_turned")
        inv_done = sem("inv_done")
        norm_turned = sem("norm_turned")
        y_done = sem("y_done")
        summed = sem("summed")
        stored = sem("stored")

        exp0, av0, copied0, turned0, summed0, stored0 = S_BANKS, NR, 1, 1, 1, 16

        block = ctx.enter_context(nc.Block())

        @block.sync
        def _(sp):
            sp.sem_inc(stored, stored0)
            def batch(b, first, last):
                for g in range(GROUPS):
                    if not (last and g > 0):
                        sp.wait_ge(av_done, SLOTS * b + HALVES * KT * g + av0)
                        maxima.load_step(sp, b + (g > 0), (g + GROUPS - 1) % GROUPS)
                    for half in range(HALVES):
                        hs = HALVES * g + half
                        if "max" in turns(hs, 2, first, last):
                            maxima.send_max(sp, 1 - half, (g + half) % GROUPS, HALF_STEPS * b + hs + 1)
                        if hs == HALVES:
                            sp.wait_ge(summed, 2 * b + summed0)
                            if not first:
                                sp.dma_start(out_v[b - 1], y_b[:]).then_inc(stored, 16)
                            sp.dma_start(x_b[:], x_v[b]).then_inc(residual_in, 16)
                            sp.dma_start(gate_b[:], gate_v[b]).then_inc(residual_in, 16)

            sp.dma_start(wo[:], w_o.rearrange("(k p) n -> p k n", p=P)).then_inc(wo_in, 16)
            batch(0, True, False)
            with sp.Fori(1, batches - 1) as b:
                batch(b, False, False)
            batch(batches - 1, False, True)
            for hq in range(2):
                sp.wait_ge(summed, 2 * batches - 1 + hq + summed0)
                tiles = slice(hq * QT, (hq + 1) * QT)
                sp.dma_start(out_v[batches - 1][:, tiles], y_b[:, tiles]).then_inc(stored, 16)
            sp.wait_ge(stored, 16 * (batches + 1) + stored0)

        @block.tensor
        def _(pe):
            pe.sem_inc(av_done, av0)

            def scores(slot, g, half, kt, j, at):
                n = PER_GROUP * at + j
                pe.wait_ge(exp_done, PER_GROUP * slot + (0 if n == 0 else j - S_BANKS + 1) + exp0)
                pe.matmul(psum[:, n % S_BANKS], maxima.k_stack[0:ROWS, g, kt * P:(kt + 1) * P],
                          maxima.q_stack[0:ROWS, g, half, j * BANK:(j + 1) * BANK],
                          start=True, stop=True).then_inc(scores_done, 1)

            def weighted_values(b, at):
                slot, kt, g = SLOTS * b + at, at % KT, at % SLOTS // KT // HALVES
                pe.wait_ge(exp_done, PER_GROUP * (slot + 1) + exp0)
                if kt == 0:
                    pe.wait_ge(o_copied, HALF_STEPS * b + at // KT + copied0)
                for j in range(PER_GROUP):
                    ins = pe.matmul(psum[32 * j:32 * j + 32, O_BANK], maxima.v_ones[:, g, kt], probs[:, kt % NR, j],
                                    start=(kt == 0), stop=(kt == KT - 1))
                ins.then_inc(av_done, 1)

            def turn(name, n_half, use, at, settled):
                bank = ring_bank(at)
                pe.wait_ge(maxima.ring_free, use - (0 if settled else 1) + ring0)
                if name == "outputs":
                    pe.wait_ge(o_copied, n_half + copied0)
                    for qt in range(QT):
                        ins = pe.transpose(psum[:, bank, qt * P:(qt + 1) * P], o_sum[:, qt * P:(qt + 1) * P], ident[:])
                    ins.then_inc(o_turned, 1)
                elif name.startswith("norm"):
                    hq = int(name[-1])
                    for k in range(2):
                        for qt in range(QT):
                            ins = pe.transpose(psum[:, bank + k, qt * P:(qt + 1) * P],
                                               o_norm[:, hq * QT + qt, k * P:(k + 1) * P], ident[:])
                    ins.then_inc(norm_turned, 1)
                else:
                    hq = int(name[-1])
                    for t in range(QT):
                        tile = hq * QT + t
                        for k in range(2):
                            ins = pe.matmul(psum[:, bank + t // 2, (t % 2) * dim:(t % 2 + 1) * dim],
                                            o_norm_t[:, k, tile * P:(tile + 1) * P], wo[:, k],
                                            start=(k == 0), stop=(k == 1))
                    ins.then_inc(y_done, 1)

            def batch(b, first, last):
                base, at = ring_start(b, first)
                for s in range(SLOTS):
                    hs, kt = s // KT, s % KT
                    g, half = hs // HALVES, hs % HALVES
                    n_half = HALF_STEPS * b + hs
                    if kt == 0:
                        pe.wait_ge(maxima.max_in[half], 3 * 16 * (GROUPS * b + g + 1) + maxima.MAX_IN0)
                        if half == 0 and has_maxima(hs, last):
                            pe.wait_ge(maxima.loaded[(g + 1) % GROUPS], 16 * maxima.LOADS * (b + 1 + (g + 1) // GROUPS))
                    late = has_maxima(hs, last) and kt > 0 and turns(hs, kt - 1, first, last)
                    second = None if turns(hs, kt, first, last) else 2
                    for j in range(PER_GROUP):
                        scores(SLOTS * b + s, g, half, kt, j, s)
                        if j == 0 and late:
                            maxima.max_scores(pe, (g + 1) % GROUPS, half, 2 * kt - 1, base + at, at)
                            at += 1
                        if j in (0, second) and has_maxima(hs, last):
                            maxima.max_scores(pe, (g + 1) % GROUPS, half, 2 * kt + (j > 0), base + at, at)
                            at += 1
                        if j == 1:
                            if s >= LAG or not first:
                                weighted_values(b, s - LAG)
                            for name in turns(hs, kt, first, last):
                                if name == "max":
                                    maxima.turn_max(pe, half, base + at, at, not has_maxima(hs, last))
                                else:
                                    turn(name, n_half, base + at, at, not has_maxima(hs, last))
                                at += 1
                return base, at

            pe.wait_ge(wo_in, 16)
            pe.wait_ge(maxima.ones_done, 2 * GROUPS)
            batch(0, True, False)
            with pe.Fori(1, batches - 1) as b:
                batch(b, False, False)
            base, at = batch(batches - 1, False, True)
            for s in range(SLOTS, SLOTS + LAG):
                weighted_values(batches - 1, s - LAG)
            for name in END:
                turn(name, HALF_STEPS * batches, base + at, at, True)
                at += 1

        @block.scalar
        def _(act):
            act.sem_inc(exp_done, exp0)
            act.sem_inc(o_copied, copied0)
            act.sem_inc(o_turned, turned0)

            def copy_outputs(n_half):
                act.wait_ge(av_done, KT * (n_half + 1) + av0)
                act.wait_ge(o_turned, n_half + turned0)
                nc.scalar.copy(o_sum[:], psum[:, O_BANK]).then_inc(o_copied, 1)

            def batch(b, first):
                for s in range(SLOTS):
                    hs, kt = s // KT, s % KT
                    slot = SLOTS * b + s
                    act.wait_ge(av_done, slot - NR + 1 + av0)
                    for j in range(PER_GROUP):
                        act.wait_ge(scores_done, PER_GROUP * slot + j + 1)
                        nc.scalar.activation(probs[:, kt % NR, j], psum[:, (PER_GROUP * s + j) % S_BANKS],
                                             ACT.Exp, scale=SCORE_SCALE).then_inc(exp_done, 1)
                        if kt == LAG - 1 and j == 2 and not (first and hs == 0):
                            copy_outputs(HALF_STEPS * b + hs - 1)

            batch(0, True)
            with act.Fori(1, batches) as b:
                batch(b, False)
            copy_outputs(HALF_STEPS * batches - 1)

        @block.vector
        def _(dve):
            def normalise(hs, n_half, use, at):
                g, half = hs // HALVES, hs % HALVES
                dve.wait_ge(maxima.ring_free, use + ring0)
                dve.wait_ge(o_turned, n_half + 1 + turned0)
                turned = psum[:, ring_bank(at)].rearrange("p (t j d) -> p t j d", j=PER_GROUP, d=2 * HEAD_DIM)
                nc.vector.reciprocal(inv_sum[:], turned[:, :, :, HEAD_DIM]).then_inc(inv_done, 1)
                dve.wait_ge(inv_done, n_half + 1)
                width = PER_GROUP * HEAD_DIM
                nc.vector.tensor_tensor(
                    o_norm[:, half * QT:(half + 1) * QT, g * width:(g + 1) * width]
                    .rearrange("p t (j d) -> p t j d", j=PER_GROUP),
                    turned[:, :, :, 0:HEAD_DIM],
                    inv_sum[:].unsqueeze(3).to_broadcast([P, QT, PER_GROUP, HEAD_DIM]),
                    ALU.mult).then_inc(maxima.ring_free, 1)

            def copy_norm(b, hq, at):
                dve.wait_ge(norm_turned, 2 * b + hq + 1)
                bank = ring_bank(at)
                nc.vector.tensor_copy(o_norm_t[:, :, hq * BANK:(hq + 1) * BANK],
                                      psum[:, bank:bank + 2]).then_inc(maxima.ring_free, 1)

            def gate(b, hq, at):
                if hq == 0:
                    dve.wait_ge(residual_in, 32 * (b + 1))
                    dve.wait_ge(stored, 16 * b + stored0)
                dve.wait_ge(y_done, 2 * b + hq + 1)
                bank, tiles = ring_bank(at), slice(hq * QT, (hq + 1) * QT)
                nc.vector.tensor_tensor(y_b[:, tiles].rearrange("p t d -> p (t d)"),
                                        psum[:, bank:bank + 2].rearrange("p a n -> p (a n)"),
                                        gate_b[:, tiles].rearrange("p t d -> p (t d)"),
                                        ALU.mult).then_inc(maxima.ring_free, 1)

            def end_of_batch(name, b, use, at):
                if name == "outputs":
                    normalise(HALF_STEPS - 1, HALF_STEPS * (b + 1) - 1, use, at)
                elif name.startswith("norm"):
                    copy_norm(b, int(name[-1]), at)
                else:
                    gate(b, int(name[-1]), at)

            def batch(b, first, last):
                base, at = ring_start(b, first)
                for s in range(SLOTS):
                    hs, kt = s // KT, s % KT
                    g, half = hs // HALVES, hs % HALVES
                    n_half = HALF_STEPS * b + hs
                    if kt == 0 and has_maxima(hs, last):
                        dve.wait_ge(maxima.max_turned, n_half + 1)
                    for j in range(2):
                        if has_maxima(hs, last):
                            unit = 2 * kt + j
                            maxima.reduce_max(dve, half, unit, UNITS * (n_half + HALVES) + unit, at)
                            at += 1
                        if j == 0:
                            for name in turns(hs, kt, first, last):
                                if name == "max":
                                    turn_use = base + at
                                    maxima.split_max(dve, 1 - half, n_half + 1, GROUPS * b + g + half, turn_use, at)
                                elif name == "outputs" and hs:
                                    normalise(hs - 1, n_half - 1, base + at, at)
                                else:
                                    end_of_batch(name, b if hs > 1 else b - 1, base + at, at)
                                at += 1
                        if "max" in turns(hs, kt, first, last) and j == 1:
                            maxima.mid_of_max(dve, 1 - half, turn_use)
                        if "max" in turns(hs, kt - 1, first, last) and j == 0:
                            maxima.low_of_max(dve, 1 - half, n_half + 1)
                return base, at

            batch(0, True, False)
            with dve.Fori(1, batches - 1) as b:
                batch(b, False, False)
            base, at = batch(batches - 1, False, True)
            for name in END:
                end_of_batch(name, batches - 1, base + at, at)
                at += 1

        @block.gpsimd
        def _(pool):
            pool.sem_inc(summed, summed0)

            def add_x(hq, use):
                pool.wait_ge(maxima.ring_free, use + 1 + ring0)
                tiles = slice(hq * QT, (hq + 1) * QT)
                nc.gpsimd.tensor_tensor(y_b[:, tiles], y_b[:, tiles], x_b[:, tiles], ALU.add).then_inc(summed, 1)

            def batch(b, last):
                base, at = ring_start(b, False)
                for hq in range(2):
                    add_x(hq, base + at + ring_use(False, last, f"project{hq}"))

            with pool.Fori(1, batches - 1) as b:
                batch(b, False)
            batch(batches - 1, True)
            base, at = ring_start(batches - 1, False)
            add_x(0, base + at + ring_use(False, True, "project0", HALF_STEPS - 1))
            add_x(1, base + at + ring_use(False, True) + END.index("project1"))


def build(nc, x, w_q, w_k, w_v, w_o, w_gate_t, w_up_t, w_down_t, out):
    batches, seq, dim = x.shape
    tokens = batches * seq
    q_parts = nc.dram_tensor("q_parts", (3, HEADS * HEAD_DIM, tokens), BF16).ap()
    k_parts = nc.dram_tensor("k_parts", (3, GROUPS * HEAD_DIM, tokens), BF16).ap()
    v_rows = nc.dram_tensor("v_rows", (tokens, GROUPS * HEAD_DIM), F32).ap()
    gate_rows = nc.dram_tensor("gate_rows", (tokens, dim), F32).ap()
    x_rows = x.rearrange("b t d -> (b t) d")
    out_rows = out.rearrange("b t d -> (b t) d")
    with ExitStack() as ctx:
        psum = ctx.enter_context(nc.psum_tensor("psum", [P, 8, BANK], F32))
        ident = ctx.enter_context(nc.sbuf_tensor("ident", [P, P], F32))
        maxima = Maxima(nc, ctx, psum, ident, q_parts, k_parts, v_rows, seq)
        ident_step = ctx.enter_context(nc.semaphore("ident_step"))
        with nc.Block() as block:
            @block.gpsimd
            def _(pool):
                nc.gpsimd.memset(ident[:], 0.0).then_inc(ident_step, 1)
                pool.wait_ge(ident_step, 1)
                nc.gpsimd.affine_select(out=ident[:], in_=ident[:], compare_op=ALU.not_equal, fill=1.0, base=0,
                                        pattern=[[-1, P]], channel_multiplier=1).then_inc(ident_step, 1)
                pool.wait_ge(ident_step, 2)
        project(nc, psum, ident, maxima, x_rows, w_q, w_k, w_v, w_gate_t, w_up_t, w_down_t,
                q_parts, k_parts, v_rows, gate_rows)
        attend(nc, psum, ident, maxima, x_rows, w_o, gate_rows, out_rows, batches)


def kernel(**inputs):
    import numpy as np
    from concourse import bacc
    from concourse.bass_utils import run_bass_kernel_spmd

    nc = bacc.Bacc("TRN2", target_bir_lowering=False, num_devices=1)
    arrays = {
        "x": inputs["L0_attn_x"], "w_q": inputs["L0_attn_Wq"], "w_k": inputs["L0_attn_Wk"],
        "w_v": inputs["L0_attn_Wv"], "w_o": inputs["L0_attn_Wo"],
        "w_gate_t": np.transpose(inputs["L0_ffn_w_gate"]), "w_up_t": np.transpose(inputs["L0_ffn_w_up"]),
        "w_down_t": np.transpose(inputs["L0_ffn_w_down"]),
    }
    arrays = {name: np.ascontiguousarray(a) for name, a in arrays.items()}
    args = [nc.dram_tensor(name, a.shape, mybir.dt.from_np(a.dtype), kind="ExternalInput").ap()
            for name, a in arrays.items()]
    out = nc.dram_tensor("out", arrays["x"].shape, F32, kind="ExternalOutput").ap()
    build(nc, *args, out)
    r = run_bass_kernel_spmd(nc, [arrays], core_ids=[0])
    return r.results[0]["out"]
```
